# Optimizing a Trainium2 kernel written in Bass

```python
import numpy as np
import jax
import jax.numpy as jnp

def _softmax(x, axis=-1):
    return jax.nn.softmax(x, axis=axis)

def _gelu(x):
    return jax.nn.gelu(x, approximate=True)

def _silu(x):
    return jax.nn.silu(x)

def _sigmoid(x):
    return jax.nn.sigmoid(x)

def _layernorm(x, axis=-1, eps=1e-05):
    m = jnp.mean(x, axis=axis, keepdims=True)
    v = jnp.var(x, axis=axis, keepdims=True)
    return (x - m) / jnp.sqrt(v + eps)

def _scatter_add(tgt, idx, src, axis=0):
    return tgt.at[idx].add(src)

def _segment_sum(src, seg, n):
    return jax.ops.segment_sum(src, seg, n)
kernel_name = 'mk_prb_d1_jaxref_r8_2dfa84'

def setup_inputs(seed: int=0):
    np.random.seed(seed)
    _w = jnp.asarray

    def _L0_attn_setup():
        import jax, jax.numpy as jnp
        import numpy as np
        D_INNER, DT_RANK, D_STATE = (256, 64, 16)
        B_SZ, L = (2, 128)
        key = jax.random.key(seed)
        ks = jax.random.split(key, 4)
        x = jax.random.normal(ks[0], (B_SZ, L, D_INNER), dtype=jnp.float32)
        W_xproj = jax.random.normal(ks[1], (DT_RANK + 2 * D_STATE, D_INNER), dtype=jnp.float32) * (1.0 / np.sqrt(D_INNER))
        W_dt = jax.random.normal(ks[2], (D_INNER, DT_RANK), dtype=jnp.float32) * (1.0 / np.sqrt(DT_RANK))
        b_dt = jax.random.normal(ks[3], (D_INNER,), dtype=jnp.float32) * 0.01
        A_log = jnp.log(jnp.broadcast_to(jnp.arange(1, D_STATE + 1, dtype=jnp.float32), (D_INNER, D_STATE)))
        D = jnp.ones((D_INNER,), dtype=jnp.float32)
        return {'x': x, 'W_xproj': W_xproj, 'W_dt': W_dt, 'b_dt': b_dt, 'A_log': A_log, 'D': D}
    _L0_attn_in = _L0_attn_setup()

    def _L0_ffn_setup():
        import jax, jax.numpy as jnp
        import numpy as np
        B, S, H = (2, 128, 256)
        E, K = (8, 2)
        F = 176
        FS = 704
        NORM_TOPK = False

        def _swiglu(x, wg, wu, wd):
            return jax.nn.silu(x @ wg) * (x @ wu) @ wd
        key = jax.random.key(seed)
        ks = jax.random.split(key, 9)
        s = 0.02
        return {'hidden_states': jax.random.normal(ks[0], (B, S, H), dtype=jnp.float32), 'Wr': jax.random.normal(ks[1], (H, E), dtype=jnp.float32) * s, 'Wg': jax.random.normal(ks[2], (E, H, F), dtype=jnp.float32) * s, 'Wu': jax.random.normal(ks[3], (E, H, F), dtype=jnp.float32) * s, 'Wd': jax.random.normal(ks[4], (E, F, H), dtype=jnp.float32) * s, 'Sg': jax.random.normal(ks[5], (H, FS), dtype=jnp.float32) * s, 'Su': jax.random.normal(ks[6], (H, FS), dtype=jnp.float32) * s, 'Sd': jax.random.normal(ks[7], (FS, H), dtype=jnp.float32) * s, 'Wsg': jax.random.normal(ks[8], (H, 1), dtype=jnp.float32) * s}
    _L0_ffn_in = _L0_ffn_setup()
    _d = {'L0_attn_x': _L0_attn_in['x'], 'L0_attn_W_xproj': _L0_attn_in['W_xproj'], 'L0_attn_W_dt': _L0_attn_in['W_dt'], 'L0_attn_b_dt': _L0_attn_in['b_dt'], 'L0_attn_A_log': _L0_attn_in['A_log'], 'L0_attn_D': _L0_attn_in['D'], 'L0_ffn_Wr': _L0_ffn_in['Wr'], 'L0_ffn_Wg': _L0_ffn_in['Wg'], 'L0_ffn_Wu': _L0_ffn_in['Wu'], 'L0_ffn_Wd': _L0_ffn_in['Wd'], 'L0_ffn_Sg': _L0_ffn_in['Sg'], 'L0_ffn_Su': _L0_ffn_in['Su'], 'L0_ffn_Sd': _L0_ffn_in['Sd'], 'L0_ffn_Wsg': _L0_ffn_in['Wsg']}
    _x0 = _d['L0_attn_x']
    _d['L0_attn_x'] = jax.random.normal(jax.random.fold_in(jax.random.key(seed), 1), (2, 512, 256), dtype=_x0.dtype)
    del _x0
    return _d

def reference(L0_attn_x, L0_attn_W_xproj, L0_attn_W_dt, L0_attn_b_dt, L0_attn_A_log, L0_attn_D, L0_ffn_Wr, L0_ffn_Wg, L0_ffn_Wu, L0_ffn_Wd, L0_ffn_Sg, L0_ffn_Su, L0_ffn_Sd, L0_ffn_Wsg):

    def _L0_attn_ref(x, W_xproj, W_dt, b_dt, A_log, D):
        import jax, jax.numpy as jnp
        import numpy as np
        D_INNER, DT_RANK, D_STATE = (256, 64, 16)
        B_SZ, L = (2, 128)
        A = -jnp.exp(A_log)
        x_dbl = jnp.einsum('bld,kd->blk', x, W_xproj)
        delta = x_dbl[..., :DT_RANK]
        Bmat = x_dbl[..., DT_RANK:DT_RANK + D_STATE]
        Cmat = x_dbl[..., DT_RANK + D_STATE:]
        delta = jax.nn.softplus(jnp.einsum('blr,dr->bld', delta, W_dt) + b_dt)
        deltaA = jnp.exp(delta[..., None] * A)
        BX = delta[..., None] * Bmat[:, :, None, :] * x[..., None]
        dA_t = jnp.moveaxis(deltaA, 1, 0)
        BX_t = jnp.moveaxis(BX, 1, 0)
        C_t = jnp.moveaxis(Cmat, 1, 0)
        h0 = jnp.zeros((x.shape[0], D_INNER, D_STATE), dtype=x.dtype)

        def step(h, inp):
            dA, bx, c = inp
            h = dA * h + bx
            y = jnp.einsum('bdn,bn->bd', h, c)
            return (h, y)
        _, ys = jax.lax.scan(step, h0, (dA_t, BX_t, C_t))
        y = jnp.moveaxis(ys, 0, 1) + D * x
        return y

    def _L0_ffn_ref(hidden_states, Wr, Wg, Wu, Wd, Sg, Su, Sd, Wsg):
        import jax, jax.numpy as jnp
        import numpy as np
        B, S, H = (2, 128, 256)
        E, K = (8, 2)
        F = 176
        FS = 704
        NORM_TOPK = False

        def _swiglu(x, wg, wu, wd):
            return jax.nn.silu(x @ wg) * (x @ wu) @ wd
        b, s, h = hidden_states.shape
        x = hidden_states.reshape(-1, h)
        router_logits = x @ Wr
        probs = jax.nn.softmax(router_logits.astype(jnp.float32), axis=-1)
        routing_weights, selected = jax.lax.top_k(probs, K)
        if NORM_TOPK:
            routing_weights = routing_weights / routing_weights.sum(-1, keepdims=True)
        routing_weights = routing_weights.astype(x.dtype)
        C = jnp.einsum('tk,tke->te', routing_weights, jax.nn.one_hot(selected, E, dtype=x.dtype))
        expert_out = jax.vmap(lambda wg, wu, wd: _swiglu(x, wg, wu, wd))(Wg, Wu, Wd)
        moe_out = jnp.einsum('te,eth->th', C, expert_out)
        shared = _swiglu(x, Sg, Su, Sd)
        shared = jax.nn.sigmoid(x @ Wsg) * shared
        out = (moe_out + shared).reshape(b, s, h)
        return out
    x = L0_attn_x
    xn = _layernorm(x, axis=-1)
    x = x + _L0_attn_ref(xn, L0_attn_W_xproj, L0_attn_W_dt, L0_attn_b_dt, L0_attn_A_log, L0_attn_D) + _L0_ffn_ref(xn, L0_ffn_Wr, L0_ffn_Wg, L0_ffn_Wu, L0_ffn_Wd, L0_ffn_Sg, L0_ffn_Su, L0_ffn_Sd, L0_ffn_Wsg)
    return x

_drawn_inputs = setup_inputs


def setup_inputs(seed=0):
    import zlib

    import numpy as np

    out = dict(_drawn_inputs(seed))
    spreads = {'L0_attn_D': (1.0, 0.6)}
    factors = {'L0_attn_b_dt': 36.513,
     'L0_ffn_Wr': 8.0,
     'L0_ffn_Wg': 8.0,
     'L0_ffn_Wu': 8.0,
     'L0_ffn_Wd': 8.0,
     'L0_ffn_Sg': 8.0,
     'L0_ffn_Su': 8.0,
     'L0_ffn_Sd': 8.0,
     'L0_ffn_Wsg': 8.0}
    for name, (base, spread) in spreads.items():
        noise = np.random.default_rng([zlib.crc32(name.encode()), seed]).standard_normal(out[name].shape)
        drawn = base * np.exp(spread * noise) if base else spread * noise
        out[name] = jnp.asarray(drawn.astype(out[name].dtype))
    for name, factor in factors.items():
        out[name] = (out[name] * factor).astype(out[name].dtype)
    return out
```

```python
from contextlib import ExitStack

import concourse.bass as bass
from concourse import mybir

ALU = mybir.AluOpType
ACT = mybir.ActivationFunctionType
AX = mybir.AxisListType
F32 = mybir.dt.float32
BF16 = mybir.dt.bfloat16

P = 128
NB = 2
L = 512
H = 256
KC = H // P
TB = L // P
NT = NB * TB
R = 64
N = 16
E = 8
FE = 176
FS = 704
F = FS + E * FE
TAIL = F - N * P
TOPK = 2
EPS = 1e-5

SM_R, SM_G, SM_B, SM_C, SM = 0, E, E + 1, E + 1 + N, E + 1 + 2 * N
SMP = 64
ST_G, ST_E, STP = N, N + 1, 32
PARTS = 3
SK = PARTS * STP

DA, HT, GB, UB, ACC = 0, 2, 4, 5, 6


def build(nc, x, wgu, wgu_tail, wd, wsm, wdel, wdt, bdt, alog, dskip, consts, selectors, out):
    ctx = ExitStack()
    with ctx:
        def sb(name, shape, dt=F32):
            return ctx.enter_context(nc.sbuf_tensor(name, shape, dt))

        def sem(name):
            return ctx.enter_context(nc.semaphore(name))

        ps = ctx.enter_context(nc.psum_tensor("ps", [P, 8, 512], F32))

        xt = sb("xt", [P, NT, H])
        xn = sb("xn", [P, NT, H])
        yacc = sb("yacc", [P, NT, H])
        xnT = sb("xnT", [P, KC, NB * L])
        delta = sb("delta", [P, KC, NB * L])
        u = sb("u", [P, KC, NB * L])
        sp_a = sb("sp_a", [P, KC, NB * L])
        dtr = sb("dtr", [R, NB, L])
        wsm_s = sb("wsm_s", [P, KC, SM])
        wdel_s = sb("wdel_s", [P, KC, R])
        wdt_s = sb("wdt_s", [R, KC, P])
        bdt_s = sb("bdt_s", [P, KC])
        A = sb("A", [P, KC * N])
        dsk = sb("dsk", [P, H])
        con = sb("con", [P, P + E * E])
        ident = con[:, 0:P]
        lower = con[:, P:P + E * E].rearrange("p (a b) -> p a b", a=E)
        sel = sb("sel", [SK, N * P + F], BF16)
        stats = sb("stats", [P, NT, 6])
        mv = sb("mv", [P, NT, 2])
        ve = sb("ve", [P, NT])
        sd = sb("sd", [P, NT])
        rs = sb("rs", [P, NT])
        rt = sb("rt", [P, NT])
        sm = sb("sm", [P, NT, SM])
        rmx = sb("rmx", [P, NT])
        lg = sb("lg", [P, NT, E + 1])
        eg = sb("eg", [P, NT, E + 1])
        rsum = sb("rsum", [P, NT, 2])
        pr = sb("pr", [P, NT, E])
        beats = sb("beats", [P, NT, E, E])
        ties = sb("ties", [P, NT, E, E])
        rank = sb("rank", [P, NT, E])
        zt = sb("zt", [P, NT, PARTS, STP])
        stack = sb("stack", [SK, NB * L], BF16)
        mid = sb("mid", [SK, L], BF16)
        rest = sb("rest", [SK, L])
        bb = sb("bb", [P, 2, L])
        bx = sb("bx", [P, 2, KC, L])
        h = sb("h", [P, 2, KC, L])
        th = sb("th", [P, 2, L])
        us = sb("us", [P, 2, L])
        cb = sb("cb", [P, 2, L])
        ag = sb("ag", [P, 2, L])
        hid = sb("hid", [P, 2, L])
        wg_r = sb("wg_r", [P, 2, 2, KC, P])
        wd_r = sb("wd_r", [P, 2, H])

        x_in = [sem(f"x_in{b}") for b in range(NB)]
        con_in = sem("con_in")
        wsm_in = sem("wsm_in")
        wdel_in = sem("wdel_in")
        wdt_in = sem("wdt_in")
        bdt_in = sem("bdt_in")
        alog_in = sem("alog_in")
        dsk_in = sem("dsk_in")
        sel_in = sem("sel_in")
        wg_in = [sem(f"wg_in{k}") for k in range(2)]
        wd_in = [sem(f"wd_in{k}") for k in range(2)]
        stored = sem("stored")
        dve_chain = sem("dve_chain")
        ve_ready = sem("ve_ready")
        sd_ready = sem("sd_ready")
        xn_ready = sem("xn_ready")
        xnT_ps = sem("xnT_ps")
        xnT_ready = [sem(f"xnT_ready{kc}") for kc in range(KC)]
        sm_ps = sem("sm_ps")
        dtr_ps = sem("dtr_ps")
        dtr_ready = sem("dtr_ready")
        z_ps = sem("z_ps")
        zpos_ready = sem("zpos_ready")
        act_chain = sem("act_chain")
        delta_log = sem("delta_log")
        delta_ready = sem("delta_ready")
        u_done = sem("u_done")
        pool_chain = sem("pool_chain")
        yinit_ready = sem("yinit_ready")
        A_exp = sem("A_exp")
        A_ready = sem("A_ready")
        lg_ready = sem("lg_ready")
        eg_ready = sem("eg_ready")
        zt_ready = sem("zt_ready")
        zt_ps = sem("zt_ps")
        stack_ready = sem("stack_ready")
        b_ps = sem("b_ps")
        b_copied = sem("b_copied")
        bx_ready = sem("bx_ready")
        c_ps = sem("c_ps")
        c_copied = sem("c_copied")
        dA_ready = sem("dA_ready")
        scanned = sem("scanned")
        hT_ready = sem("hT_ready")
        y_added = sem("y_added")
        g_ready = sem("g_ready")
        u_ready = sem("u_ready")
        tanh_ready = sem("tanh_ready")
        us_ready = sem("us_ready")
        ag_ready = sem("ag_ready")
        q_ready = sem("q_ready")
        hid_ready = sem("hid_ready")
        down_done = sem("down_done")
        y_final = sem("y_final")

        hT = ps[:, HT:HT + 2, :].rearrange("p a (j d) -> p (a j) d", d=H)
        acc = ps[:, ACC:ACC + 2, :].rearrange("p a (j d) -> p (a j) d", d=H)

        def state(b, n0, i):
            return N * b + n0 + 2 * i

        def chunk(b, n0, i):
            return (N + 1) * b + n0 + 2 * i

        def chunk_slot(b, n0):
            return ((N + 1) * b + n0) % 2

        def chunk_use(b, n0, i):
            return ((N + 1) * b + n0) // 2 + i + 1

        def steps(eng, b, step, tail):
            step(b, 0, 0)
            step(b, 1, 0)
            with eng.Fori(0, N // 2 - 2) as i:
                step(b, 2, i)
                step(b, 3, i)
            step(b, N - 2, 0)
            step(b, N - 1, 0)
            tail(b)

        block = ctx.enter_context(nc.Block())

        @block.sync
        def _(sp):
            xv = x.rearrange("(t p) d -> p t d", p=P)
            ov = out.rearrange("(t p) d -> p t d", p=P)
            for b in range(NB):
                sp.dma_start(xt[:, TB * b:TB * b + TB, :], xv[:, TB * b:TB * b + TB, :]).then_inc(x_in[b], 16)
                if b == 0:
                    sp.dma_start(con[:, :], consts).then_inc(con_in, 16)
            sp.dma_start(wdel_s[:, :, :], wdel).then_inc(wdel_in, 16)
            sp.dma_start(wsm_s[:, :, :], wsm).then_inc(wsm_in, 16)
            sp.dma_start(wdt_s[:, :, :], wdt).then_inc(wdt_in, 16)

            def load(b, n0, i):
                m, slot = chunk(b, n0, i), chunk_slot(b, n0)
                first = b == 0 and n0 < 2
                n = n0 + 2 * i
                if not first:
                    sp.wait_ge(u_ready, m - 1)
                if isinstance(n, int) and n == N:
                    sp.dma_start(wg_r[:, slot, :, :, 0:TAIL], wgu_tail).then_inc(wg_in[slot], 16)
                else:
                    src = wgu[bass.ds(n, 1)].rearrange("a p g k f -> (a p) g k f")
                    sp.dma_start(wg_r[:, slot, :, :, :], src).then_inc(wg_in[slot], 16)
                if not first:
                    sp.wait_ge(down_done, m - 1)
                if isinstance(n, int) and n == N:
                    sp.dma_start(wd_r[0:TAIL, slot, :], wd[N * P:F, :]).then_inc(wd_in[slot], 16)
                else:
                    sp.dma_start(wd_r[:, slot, :], wd[bass.ds(n * P, P), :]).then_inc(wd_in[slot], 16)

            def store(b):
                sp.wait_ge(y_final, 2 * (b + 1))
                sp.dma_start(ov[:, TB * b:TB * b + TB, :], yacc[:, TB * b:TB * b + TB, :]).then_inc(stored, 16)

            for b in range(NB):
                load(b, 0, 0)
                load(b, 1, 0)
                if b:
                    store(b - 1)
                with sp.Fori(0, N // 2 - 1) as i:
                    load(b, 2, i)
                    load(b, 3, i)
                load(b, N, 0)
            store(NB - 1)
            sp.wait_ge(stored, 16 * NB)

        @block.gpsimd
        def _(pool):
            chain = [0]

            def link(ins):
                chain[0] += 1
                ins.then_inc(pool_chain, 1)
                pool.wait_ge(pool_chain, chain[0])

            pool.wait_ge(dsk_in, 16)
            for b in range(NB):
                t = slice(TB * b, TB * b + TB)
                pool.wait_ge(xn_ready, b + 1)
                link(pool.tensor_tensor(yacc[:, t, :], xn[:, t, :], dsk[:, None, :].to_broadcast([P, TB, H]), ALU.mult))
                pool.tensor_tensor(yacc[:, t, :], yacc[:, t, :], xt[:, t, :], ALU.add).then_inc(yinit_ready, 1)
            for b in range(NB):
                c = slice(L * b, L * b + L)
                pool.wait_ge(delta_ready, b + 1)
                for kc in range(KC):
                    pool.wait_ge(xnT_ready[kc], b + 1)
                pool.tensor_tensor(u[:, :, c], delta[:, :, c], xnT[:, :, c], ALU.mult).then_inc(u_done, 1)

            def drive(b, n0, i):
                s = state(b, n0, i)
                slot = n0 % 2
                pool.wait_ge(b_copied, s + 1)
                if b == 0 and n0 < 2:
                    pool.wait_ge(u_done, NB)
                else:
                    pool.wait_ge(scanned, KC * (s - 1))
                bs = bb[:, slot, :]
                pool.tensor_tensor(bx[:, slot, :, :], u[:, :, L * b:L * b + L],
                                   bs[:, None, :].to_broadcast([P, KC, L]), ALU.mult).then_inc(bx_ready, 1)

            def hidden(b, n0, i, rows):
                m, slot = chunk(b, n0, i), chunk_slot(b, n0)
                start = b == 0 and n0 == 0
                r = slice(0, rows)
                pool.wait_ge(us_ready, m + 1)
                pool.wait_ge(c_copied, m + 1)
                pool.tensor_tensor(us[r, slot, :], us[r, slot, :], cb[r, slot, :], ALU.mult).then_inc(q_ready, 1)
                pool.wait_ge(q_ready, m + 1)
                pool.wait_ge(ag_ready, m + 1)
                if not start:
                    pool.wait_ge(down_done, m - 1)
                pool.tensor_tensor(hid[r, slot, :], ag[r, slot, :], us[r, slot, :], ALU.mult).then_inc(hid_ready, 1)

            def step(b, n0, i):
                if n0 == N - 1:
                    if b + 1 < NB:
                        drive(b + 1, 0, 0)
                else:
                    drive(b, n0 + 1, i)
                hidden(b, n0, i, P)

            drive(0, 0, 0)
            for b in range(NB):
                steps(pool, b, step, lambda b: hidden(b, N, 0, TAIL))

        @block.scalar
        def _(act):
            act.dma_start(bdt_s[:, :], bdt).then_inc(bdt_in, 16)
            act.dma_start(A[:, :], alog).then_inc(alog_in, 16)
            act.dma_start(dsk[:, :], dskip[None, :].to_broadcast([P, H])).then_inc(dsk_in, 16)
            act.dma_start(sel[:, :], selectors).then_inc(sel_in, 16)
            for b in range(NB):
                t = slice(TB * b, TB * b + TB)
                act.wait_ge(ve_ready, b + 1)
                act.activation(sd[:, t], ve[:, t], ACT.Sqrt).then_inc(sd_ready, 1)
            act.wait_ge(alog_in, 16)
            act.activation(A[:, :], A[:, :], ACT.Exp).then_inc(A_exp, 1)
            for b in range(NB):
                act.wait_ge(xnT_ps, b + 1)
                act.activation(xnT[:, 1, L * b:L * b + L], ps[:, 2 * b + 1, :], ACT.Copy)\
                   .then_inc(xnT_ready[1], 1)
                act.wait_ge(dtr_ps, b + 1)
                act.activation(dtr[:, b, :], ps[0:R, 4 + b, :], ACT.Copy).then_inc(dtr_ready, 1)
            act.wait_ge(bdt_in, 16)
            for b in range(NB):
                act.wait_ge(z_ps, b + 1)
                for kc in range(KC):
                    act.activation(sp_a[:, kc, L * b:L * b + L], ps[:, 2 * b + kc, :], ACT.Abs,
                                   bias=bdt_s[:, kc:kc + 1]).then_inc(act_chain, 1)
                act.wait_ge(act_chain, 3 * b + 2)
                act.activation(sp_a[:, :, L * b:L * b + L], sp_a[:, :, L * b:L * b + L], ACT.Exp, scale=-1.0)\
                   .then_inc(act_chain, 1)
            act.wait_ge(lg_ready, 1)
            act.activation(eg[:, :, :], lg[:, :, :], ACT.Exp).then_inc(eg_ready, 1)
            act.wait_ge(act_chain, 3 * NB)
            for b in range(NB):
                act.activation(sp_a[:, :, L * b:L * b + L], sp_a[:, :, L * b:L * b + L], ACT.Ln, bias=1.0)\
                   .then_inc(delta_log, 1)

            def b_copy(b, n0, i):
                s = state(b, n0, i)
                act.wait_ge(b_ps, s + 1)
                if not (b == 0 and n0 == 0):
                    act.wait_ge(bx_ready, s - 1)
                act.activation(bb[:, n0 % 2, :], ps[:, GB, :], ACT.Copy).then_inc(b_copied, 1)

            def decay(b, n0, i, kc):
                s = state(b, n0, i)
                if b == 0 and n0 == 0:
                    act.wait_ge(delta_ready, NB)
                    act.wait_ge(A_ready, 1)
                else:
                    act.wait_ge(scanned, KC * (s - 1) + kc + 1)
                n = n0 + 2 * i
                act.activation(ps[:, DA + kc, :], delta[:, kc, L * b:L * b + L], ACT.Exp,
                               scale=A[:, bass.ds(kc * N + n, 1)]).then_inc(dA_ready, 1)

            def c_copy(b, n0, i, rows):
                m, slot = chunk(b, n0, i), chunk_slot(b, n0)
                act.wait_ge(c_ps, m + 1)
                if not (b == 0 and n0 == 0):
                    act.wait_ge(q_ready, m - 1)
                act.activation(cb[0:rows, slot, :], ps[0:rows, UB, :], ACT.Copy).then_inc(c_copied, 1)

            def gate_up(b, n0, i, rows):
                m, slot = chunk(b, n0, i), chunk_slot(b, n0)
                act.wait_ge(g_ready, m + 1)
                if not (b == 0 and n0 == 0):
                    act.wait_ge(ag_ready, m - 1)
                act.activation(th[0:rows, slot, :], ps[0:rows, GB, :], ACT.Tanh, scale=0.5).then_inc(tanh_ready, 1)
                act.wait_ge(u_ready, m + 1)
                if not (b == 0 and n0 == 0):
                    act.wait_ge(hid_ready, m - 1)
                act.activation(us[0:rows, slot, :], ps[0:rows, UB, :], ACT.Copy, scale=0.5).then_inc(us_ready, 1)

            def step(b, n0, i):
                if n0 == N - 1:
                    if b + 1 < NB:
                        b_copy(b + 1, 0, 0)
                else:
                    b_copy(b, n0 + 1, i)
                decay(b, n0, i, 0)
                c_copy(b, n0, i, P)
                decay(b, n0, i, 1)
                gate_up(b, n0, i, P)

            def tail(b):
                c_copy(b, N, 0, TAIL)
                gate_up(b, N, 0, TAIL)

            b_copy(0, 0, 0)
            for b in range(NB):
                steps(act, b, step, tail)

        @block.vector
        def _(dve):
            chain = [0]

            def link(ins):
                chain[0] += 1
                ins.then_inc(dve_chain, 1)
                dve.wait_ge(dve_chain, chain[0])

            link(dve.memset(zt[:, :, :, :], 0.0))
            for b in range(NB):
                t = slice(TB * b, TB * b + TB)
                dve.wait_ge(x_in[b], 16)
                for k in range(TB * b, TB * b + TB):
                    last = dve.bn_stats(stats[:, k, :], xt[:, k, :])
                link(last)
                for k in range(TB * b, TB * b + TB):
                    last = dve.bn_aggr(mv[:, k, :], stats[:, k, :])
                link(last)
                dve.tensor_scalar(ve[:, t], mv[:, t, 1], EPS, None, ALU.add).then_inc(ve_ready, 1)
            for b in range(NB):
                t = slice(TB * b, TB * b + TB)
                dve.wait_ge(sd_ready, b + 1)
                link(dve.reciprocal(rs[:, t], sd[:, t]))
                link(dve.tensor_tensor(rt[:, t], rs[:, t], rs[:, t], ALU.mult))
                link(dve.tensor_tensor(rt[:, t], rt[:, t], ve[:, t], ALU.mult))
                link(dve.tensor_scalar(rt[:, t], rt[:, t], -0.5, 1.5, ALU.mult, ALU.add))
                link(dve.tensor_tensor(rs[:, t], rs[:, t], rt[:, t], ALU.mult))
                for k in range(TB * b, TB * b + TB):
                    last = dve.tensor_scalar(xn[:, k, :], xt[:, k, :], mv[:, k, 0:1], rs[:, k:k + 1],
                                             ALU.subtract, ALU.mult)
                last.then_inc(xn_ready, 1)
            for b in range(NB):
                dve.wait_ge(xnT_ps, b + 1)
                dve.tensor_copy(xnT[:, 0, L * b:L * b + L], ps[:, 2 * b, :]).then_inc(xnT_ready[0], 1)
            dve.wait_ge(A_exp, 1)
            dve.tensor_scalar(A[:, :], A[:, :], -1.0, None, ALU.mult).then_inc(A_ready, 1)
            dve.wait_ge(bdt_in, 16)
            for b in range(NB):
                dve.wait_ge(act_chain, 3 * b + 2)
                for kc in range(KC):
                    last = dve.tensor_scalar(delta[:, kc, L * b:L * b + L], ps[:, 2 * b + kc, :],
                                             bdt_s[:, kc:kc + 1], 0.0, ALU.add, ALU.max)
                link(last)
            dve.wait_ge(sm_ps, NT)
            link(dve.tensor_copy(sm[:, :, :], ps[:, 6, :].rearrange("p (t c) -> p t c", c=SMP)[:, :, 0:SM]))
            link(dve.tensor_reduce(rmx[:, :], sm[:, :, SM_R:SM_R + E], AX.X, ALU.max))
            dve.tensor_tensor(lg[:, :, 0:E], sm[:, :, SM_R:SM_R + E], rmx[:, :, None].to_broadcast([P, NT, E]),
                              ALU.subtract)
            dve.tensor_scalar(lg[:, :, E], sm[:, :, SM_G], -1.0, 80.0, ALU.mult, ALU.min).then_inc(lg_ready, 1)
            dve.tensor_copy(zt[:, :, :, 0:N], sm[:, :, None, SM_B:SM_B + N].to_broadcast([P, NT, PARTS, N]))
            dve.wait_ge(eg_ready, 1)
            dve.tensor_reduce(rsum[:, :, 0], eg[:, :, 0:E], AX.X, ALU.add)
            link(dve.tensor_scalar(rsum[:, :, 1], eg[:, :, E], 1.0, None, ALU.add))
            link(dve.reciprocal(rsum[:, :, :], rsum[:, :, :]))
            dve.tensor_copy(zt[:, :, :, ST_G], rsum[:, :, 1:2].to_broadcast([P, NT, PARTS]))
            link(dve.tensor_tensor(pr[:, :, :], eg[:, :, 0:E], rsum[:, :, 0:1].to_broadcast([P, NT, E]), ALU.mult))
            other = pr[:, :, None, :].to_broadcast([P, NT, E, E])
            own = pr[:, :, :, None].to_broadcast([P, NT, E, E])
            dve.tensor_tensor(beats[:, :, :, :], other, own, ALU.is_gt)
            link(dve.tensor_tensor(ties[:, :, :, :], other, own, ALU.is_equal))
            link(dve.tensor_tensor(ties[:, :, :, :], ties[:, :, :, :],
                                   lower[:, None, :, :].to_broadcast([P, NT, E, E]), ALU.mult))
            link(dve.tensor_tensor(beats[:, :, :, :], beats[:, :, :, :], ties[:, :, :, :], ALU.add))
            link(dve.tensor_reduce(rank[:, :, :], beats[:, :, :, :], AX.X, ALU.add))
            link(dve.tensor_scalar(rank[:, :, :], rank[:, :, :], float(TOPK), None, ALU.is_lt))
            link(dve.tensor_tensor(pr[:, :, :], pr[:, :, :], rank[:, :, :], ALU.mult))
            dve.tensor_copy(zt[:, :, :, ST_E:ST_E + E], pr[:, :, None, :].to_broadcast([P, NT, PARTS, E]))\
               .then_inc(zt_ready, 1)
            for b in range(NB):
                dve.wait_ge(delta_log, b + 1)
                c = slice(L * b, L * b + L)
                dve.tensor_tensor(delta[:, :, c], delta[:, :, c], sp_a[:, :, c], ALU.add).then_inc(delta_ready, 1)
            for b in range(NB):
                c = slice(L * b, L * b + L)
                dve.wait_ge(zt_ps, b + 1)
                zp = ps[0:SK, 7 - b, :]
                link(dve.tensor_copy(stack[:, c], zp))
                link(dve.tensor_tensor(rest[:, :], zp, stack[:, c], ALU.subtract))
                link(dve.tensor_copy(mid[:, :], rest[:, :]))
                link(dve.tensor_tensor(rest[:, :], rest[:, :], mid[:, :], ALU.subtract))
                dve.tensor_copy(stack[STP:2 * STP, c], mid[STP:2 * STP, :])
                dve.tensor_copy(stack[2 * STP:SK, c], rest[2 * STP:SK, :]).then_inc(stack_ready, 1)
                dve.wait_ge(stack_ready, b + 1)

            def add_y(b, n0, i):
                s = state(b, n0, i)
                n = n0 + 2 * i
                dve.wait_ge(hT_ready, s + 1)
                if b == 0 and n0 == 0:
                    dve.wait_ge(yinit_ready, NB)
                else:
                    dve.wait_ge(y_added, s)
                for j in range(TB):
                    t = TB * b + j
                    last = dve.scalar_tensor_tensor(yacc[:, t, :], hT[:, j, :], sm[:, t, bass.ds(SM_C + n, 1)],
                                                    yacc[:, t, :], ALU.mult, ALU.add)
                last.then_inc(y_added, 1)

            def silu(b, n0, i, rows):
                m, slot = chunk(b, n0, i), chunk_slot(b, n0)
                dve.wait_ge(tanh_ready, m + 1)
                if not (b == 0 and n0 == 0):
                    dve.wait_ge(hid_ready, m - 1)
                dve.scalar_tensor_tensor(ag[0:rows, slot, :], th[0:rows, slot, :], 1.0, ps[0:rows, GB, :],
                                         ALU.add, ALU.mult).then_inc(ag_ready, 1)

            def scan(b, n0, i):
                s = state(b, n0, i)
                slot = n0 % 2
                dve.wait_ge(bx_ready, s + 1)
                for kc in range(KC):
                    dve.wait_ge(dA_ready, KC * s + kc + 1)
                    dve.tensor_tensor_scan(h[:, slot, kc, :], ps[:, DA + kc, :], bx[:, slot, kc, :], 0.0,
                                           ALU.mult, ALU.add).then_inc(scanned, 1)

            def step(b, n0, i):
                if n0 > 0:
                    add_y(b, n0 - 1, i)
                scan(b, n0, i)
                silu(b, n0, i, P)

            def tail(b):
                add_y(b, N - 1, 0)
                silu(b, N, 0, TAIL)
                dve.wait_ge(y_added, N * (b + 1))
                dve.wait_ge(down_done, (N + 1) * (b + 1))
                for k in range(2):
                    t = slice(TB * b + 2 * k, TB * b + 2 * k + 2)
                    dve.tensor_tensor(yacc[:, t, :], yacc[:, t, :], acc[:, 2 * k:2 * k + 2, :], ALU.add)\
                       .then_inc(y_final, 1)

            for b in range(NB):
                steps(dve, b, step, tail)

        @block.tensor
        def _(pe):
            pe.wait_ge(con_in, 16)
            for b in range(NB):
                pe.wait_ge(xn_ready, b + 1)
                for kc in range(KC):
                    for j in range(TB):
                        last = pe.transpose(ps[:, 2 * b + kc, j * P:(j + 1) * P],
                                            xn[:, TB * b + j, kc * P:(kc + 1) * P], ident)
                last.then_inc(xnT_ps, 1)
            for b in range(NB):
                pe.wait_ge(wdel_in, 16)
                for kc in range(KC):
                    pe.wait_ge(xnT_ready[kc], b + 1)
                for kc in range(KC):
                    last = pe.matmul(ps[0:R, 4 + b, :], wdel_s[:, kc, :], xnT[:, kc, L * b:L * b + L],
                                     start=kc == 0, stop=kc == KC - 1)
                last.then_inc(dtr_ps, 1)
            pe.wait_ge(wsm_in, 16)
            for t in range(NT):
                for kc in range(KC):
                    last = pe.matmul(ps[:, 6, SMP * t:SMP * t + SM], xnT[:, kc, t * P:(t + 1) * P],
                                     wsm_s[:, kc, :], start=kc == 0, stop=kc == KC - 1)
                last.then_inc(sm_ps, 1)
            pe.wait_ge(wdt_in, 16)
            for b in range(NB):
                pe.wait_ge(dtr_ready, b + 1)
                for kc in range(KC):
                    last = pe.matmul(ps[:, 2 * b + kc, :], wdt_s[:, kc, :], dtr[:, b, :], start=True, stop=True)
                last.then_inc(z_ps, 1)
            pe.wait_ge(zt_ready, 1)
            for b in range(NB):
                for j in range(TB):
                    last = pe.transpose(ps[0:SK, 7 - b, j * P:(j + 1) * P],
                                        zt[:, TB * b + j, :, :].rearrange("p a c -> p (a c)"), ident)
                last.then_inc(zt_ps, 1)

            def spread_b(b, n0, i):
                n, m = n0 + 2 * i, chunk(b, n0, i) - 1
                if b == 0 and n0 == 0:
                    pe.wait_ge(stack_ready, NB)
                    pe.wait_ge(sel_in, 16)
                    pe.wait_ge(dtr_ready, NB)
                elif n0 == 0:
                    pe.wait_ge(ag_ready, (N + 1) * b - 2)
                elif not (b == 0 and n0 == 1):
                    pe.wait_ge(ag_ready, m)
                else:
                    pe.wait_ge(b_copied, 1)
                pe.matmul(ps[:, GB, :], sel[:, bass.ds(n * P, P)], stack[:, L * b:L * b + L],
                          start=True, stop=True).then_inc(b_ps, 1)

            def spread_c(b, n0, i, rows):
                m, n = chunk(b, n0, i), n0 + 2 * i
                if not (b == 0 and n0 == 0):
                    pe.wait_ge(us_ready, m)
                pe.matmul(ps[0:rows, UB, :], sel[:, bass.ds(N * P + n * P, rows)], stack[:, L * b:L * b + L],
                          start=True, stop=True).then_inc(c_ps, 1)

            def turn_h(b, n0, i):
                s, slot = state(b, n0, i), n0 % 2
                pe.wait_ge(scanned, KC * (s + 1))
                if not (b == 0 and n0 == 0):
                    pe.wait_ge(y_added, s)
                for j in range(TB):
                    for kc in range(KC):
                        last = pe.transpose(hT[:, j, kc * P:(kc + 1) * P], h[:, slot, kc, j * P:(j + 1) * P], ident)
                last.then_inc(hT_ready, 1)

            def project(b, n0, i, which, rows):
                slot = chunk_slot(b, n0)
                bank, done = ((GB, g_ready), (UB, u_ready))[which]
                for kc in range(KC):
                    last = pe.matmul(ps[0:rows, bank, :], wg_r[:, slot, which, kc, 0:rows],
                                     xnT[:, kc, L * b:L * b + L], start=kc == 0, stop=kc == KC - 1)
                last.then_inc(done, 1)

            def down(b, n0, i, rows):
                m, slot = chunk(b, n0, i), chunk_slot(b, n0)
                first = n0 == 0
                pe.wait_ge(hid_ready, m + 1)
                pe.wait_ge(wd_in[slot], 16 * chunk_use(b, n0, i))
                if first and b:
                    pe.wait_ge(y_final, 2 * b)
                for j in range(TB):
                    last = pe.matmul(acc[:, j, :], hid[0:rows, slot, j * P:(j + 1) * P], wd_r[0:rows, slot, :],
                                     start=first and j % 2 == 0, stop=True, skip_group_check=True)
                last.then_inc(down_done, 1)

            def step(b, n0, i):
                m, s, slot = chunk(b, n0, i), state(b, n0, i), chunk_slot(b, n0)
                if n0 < N - 1:
                    spread_b(b, n0 + 1, i)
                elif b + 1 < NB:
                    spread_b(b + 1, 0, 0)
                spread_c(b, n0, i, P)
                if n0 > 0:
                    turn_h(b, n0 - 1, i)
                if n0 == N - 1 and b + 1 == NB:
                    pe.wait_ge(ag_ready, m)
                else:
                    pe.wait_ge(b_copied, s + 2)
                pe.wait_ge(wg_in[slot], 16 * chunk_use(b, n0, i))
                project(b, n0, i, 0, P)
                if n0 > 0:
                    down(b, n0 - 1, i, P)
                pe.wait_ge(c_copied, m + 1)
                project(b, n0, i, 1, P)

            def tail(b):
                m, slot = chunk(b, N, 0), chunk_slot(b, N)
                turn_h(b, N - 1, 0)
                spread_c(b, N, 0, TAIL)
                pe.wait_ge(ag_ready, m)
                pe.wait_ge(wg_in[slot], 16 * chunk_use(b, N, 0))
                project(b, N, 0, 0, TAIL)
                down(b, N - 1, 0, P)
                pe.wait_ge(c_copied, m + 1)
                project(b, N, 0, 1, TAIL)
                down(b, N, 0, TAIL)

            spread_b(0, 0, 0)
            for b in range(NB):
                steps(pe, b, step, tail)


def kernel(L0_attn_x, L0_attn_W_xproj, L0_attn_W_dt, L0_attn_b_dt, L0_attn_A_log, L0_attn_D, L0_ffn_Wr,
           L0_ffn_Wg, L0_ffn_Wu, L0_ffn_Wd, L0_ffn_Sg, L0_ffn_Su, L0_ffn_Sd, L0_ffn_Wsg):
    import ml_dtypes
    import numpy as np
    import concourse.bacc as bacc
    from concourse.bass_utils import run_bass_kernel_spmd

    def f(a):
        return np.asarray(a)

    wx = f(L0_attn_W_xproj)
    gate = np.concatenate([f(L0_ffn_Sg), f(L0_ffn_Wg).transpose(1, 0, 2).reshape(H, E * FE)], axis=1)
    up = np.concatenate([f(L0_ffn_Su), f(L0_ffn_Wu).transpose(1, 0, 2).reshape(H, E * FE)], axis=1)
    gu = np.stack([gate, up]).reshape(2, KC, P, F).transpose(2, 0, 1, 3)
    consts = np.concatenate([np.eye(P, dtype=np.float32),
                             np.tile(np.tril(np.ones((E, E), np.float32), -1).reshape(1, E * E), (P, 1))], axis=1)
    unit = np.arange(F)
    owner = np.where(unit < FS, ST_G, ST_E + (unit - FS) // FE)
    picked = np.concatenate([np.repeat(np.arange(N), P), owner])
    selectors = (np.arange(SK)[:, None] % STP == picked[None, :]).astype(ml_dtypes.bfloat16)

    arrays = {
        "x": f(L0_attn_x).reshape(NB * L, H),
        "wgu": gu[..., :N * P].reshape(P, 2, KC, N, P).transpose(3, 0, 1, 2, 4),
        "wgu_tail": gu[..., N * P:],
        "wd": np.concatenate([f(L0_ffn_Sd), f(L0_ffn_Wd).reshape(E * FE, H)], axis=0),
        "wsm": np.concatenate([f(L0_ffn_Wr), f(L0_ffn_Wsg), wx[R:].T], axis=1).reshape(KC, P, SM).transpose(1, 0, 2),
        "wdel": wx[:R].T.reshape(KC, P, R).transpose(1, 0, 2),
        "wdt": f(L0_attn_W_dt).T.reshape(R, KC, P),
        "bdt": f(L0_attn_b_dt).reshape(KC, P).T,
        "alog": f(L0_attn_A_log).reshape(KC, P, N).transpose(1, 0, 2).reshape(P, KC * N),
        "dskip": f(L0_attn_D),
        "consts": consts,
        "selectors": selectors,
    }
    arrays = {k: np.ascontiguousarray(v) for k, v in arrays.items()}
    nc = bacc.Bacc("TRN2", target_bir_lowering=False, num_devices=1)
    args = {k: nc.dram_tensor(k, v.shape, mybir.dt.from_np(v.dtype), kind="ExternalInput").ap()
            for k, v in arrays.items()}
    args["out"] = nc.dram_tensor("out", (NB * L, H), F32, kind="ExternalOutput").ap()
    build(nc, **args)
    r = run_bass_kernel_spmd(nc, [arrays], core_ids=[0])
    return r.results[0]["out"].reshape(NB, L, H)
```

```python
from contextlib import ExitStack

import concourse.bass as bass
from concourse import mybir

ALU = mybir.AluOpType
ACT = mybir.ActivationFunctionType
AX = mybir.AxisListType
F32 = mybir.dt.float32
F32R = mybir.dt.float32r
BF16 = mybir.dt.bfloat16

P = 128
NB = 2
L = 512
H = 256
KC = H // P
TB = L // P
NT = NB * TB
R = 64
N = 16
E = 8
FE = 176
FS = 704
F = FS + E * FE
TAIL = F - N * P
TOPK = 2
EPS = 1e-5

SM_R, SM_G, SM_C, SM, SMP = 0, E, E + 1, E + 1 + N, 32
PARTS, STP = 3, 32
SK = PARTS * STP
WARM = 16

DA, HT, GB, UB, ACC = 0, 2, 4, 5, 6


def build(nc, x, wgu, wgu_tail, wd, wsm, wdel, wb, wdt, bdt, alog, dskip, consts, selectors, out):
    ctx = ExitStack()
    with ctx:
        def sb(name, shape, dt=F32):
            return ctx.enter_context(nc.sbuf_tensor(name, shape, dt))

        def sem(name):
            return ctx.enter_context(nc.semaphore(name))

        def sems(name, n):
            return [sem(f"{name}{k}") for k in range(n)]

        ps = ctx.enter_context(nc.psum_tensor("ps", [P, 8, 512], F32))

        xt = sb("xt", [P, NT, H])
        xn = sb("xn", [P, NT, H])
        yacc = sb("yacc", [P, NT, H])
        xnT = sb("xnT", [P, KC, NB * L])
        xh = sb("xh", [P, KC, NB * L], F32R)
        xl = sb("xl", [P, KC, NB * L], F32R)
        delta = sb("delta", [P, KC, NB * L])
        u = sb("u", [P, KC, NB * L])
        soft = sb("soft", [P, KC, NB * L])
        dtr = sb("dtr", [R, NB, L])
        wsm_s = sb("wsm_s", [P, KC, SM])
        wdel_s = sb("wdel_s", [P, KC, R])
        wb_s = sb("wb_s", [P, KC, SK])
        wdt_s = sb("wdt_s", [R, KC, P])
        bdt_s = sb("bdt_s", [P, KC])
        dsk_s = sb("dsk_s", [P, KC])
        A = sb("A", [P, KC * N])
        dd = sb("dd", [P, KC, P])
        warm = sb("warm", [P, L], BF16)
        con = sb("con", [P, P + E * E])
        ident = con[:, 0:P]
        lower = con[:, P:P + E * E].rearrange("p (a b) -> p a b", a=E)
        sel = sb("sel", [SK, N * P + F], BF16)
        stats = sb("stats", [P, NT, 6])
        mv = sb("mv", [P, NT, 2])
        ve = sb("ve", [P, NT])
        sd = sb("sd", [P, NT])
        rs = sb("rs", [P, NT])
        rt = sb("rt", [P, NT])
        nm = sb("nm", [P, NT])
        sm = sb("sm", [P, NT, SM])
        rmx = sb("rmx", [P, NT])
        lg = sb("lg", [P, NT, E + 1])
        eg = sb("eg", [P, NT, E + 1])
        rsum = sb("rsum", [P, NT, 2])
        pr = sb("pr", [P, NT, E])
        beats = sb("beats", [P, TB, E, E])
        ties = sb("ties", [P, TB, E, E])
        rank = sb("rank", [P, TB, E])
        zt = sb("zt", [P, NT, PARTS, STP])
        raw = sb("raw", [SK, NB, 2, L])
        stack = sb("stack", [SK, NB, 2, L], BF16)
        mid = sb("mid", [SK, L], BF16)
        rest = sb("rest", [SK, L])
        mid_b = sb("mid_b", [SK, L], BF16)
        rest_b = sb("rest_b", [SK, L])
        bb = sb("bb", [P, 2, L])
        bx = sb("bx", [P, 2, KC, L])
        h = sb("h", [P, 2, KC, L])
        th = sb("th", [P, 2, L])
        us = sb("us", [P, 2, L])
        cb = sb("cb", [P, 2, L])
        ag = sb("ag", [P, 2, L])
        hid = sb("hid", [P, 2, L])
        wg_r = sb("wg_r", [P, 2, 2, KC, P])
        wg_h = sb("wg_h", [P, 2, 2, KC, P], F32R)
        wg_l = sb("wg_l", [P, 2, 2, KC, P], F32R)
        wd_r = sb("wd_r", [P, 2, H])

        x_in = sems("x_in", NB)
        con_in, wsm_in, wdel_in, wb_in, wdt_in = map(sem, ("con_in", "wsm_in", "wdel_in", "wb_in", "wdt_in"))
        bdt_in, alog_in, dsk_in, sel_in = map(sem, ("bdt_in", "alog_in", "dsk_in", "sel_in"))
        wg_in = sems("wg_in", 2)
        wd_in = sems("wd_in", 2)
        stored = sem("stored")
        dve_chain = sem("dve_chain")
        act_chain = sem("act_chain")
        pool_chain = sem("pool_chain")
        ve_ready = sem("ve_ready")
        sd_ready = sem("sd_ready")
        nm_ready = sem("nm_ready")
        xn_dve = sem("xn_dve")
        xn_act = sem("xn_act")
        xnT_ps = sem("xnT_ps")
        xnT_ready = sems("xnT_ready", KC)
        xh_ready = sem("xh_ready")
        xl_ready = sem("xl_ready")
        sm_ps = sem("sm_ps")
        dtr_ps = sem("dtr_ps")
        dtr_first = sem("dtr_first")
        dtr_ready = sem("dtr_ready")
        rb_ps = sem("rb_ps")
        rb_ready = sem("rb_ready")
        z_ps = sem("z_ps")
        z_abs = sem("z_abs")
        z_pos = sem("z_pos")
        soft_ready = sem("soft_ready")
        delta_ready = sem("delta_ready")
        u_written = sems("u_written", NB)
        dd_ready = sem("dd_ready")
        warm_ready = sem("warm_ready")
        zt_zero = sem("zt_zero")
        A_exp = sem("A_exp")
        A_ready = sem("A_ready")
        lg_ready = sem("lg_ready")
        eg_ready = sem("eg_ready")
        zt_ready = sem("zt_ready")
        zt_ps = sem("zt_ps")
        rc_ready = sem("rc_ready")
        sm_copied = sem("sm_copied")
        stack_b = sem("stack_b")
        stack_c = sem("stack_c")
        b_ps = sem("b_ps")
        b_copied = sem("b_copied")
        bx_ready = sem("bx_ready")
        c_ps = sem("c_ps")
        c_copied = sem("c_copied")
        dA_ready = sem("dA_ready")
        scanned = sem("scanned")
        hT_ready = sem("hT_ready")
        y_added = sem("y_added")
        wh_ready = sem("wh_ready")
        wl_first = sems("wl_first", 2)
        wl_ready = sem("wl_ready")
        g_ready = sem("g_ready")
        u_ready = sem("u_ready")
        tanh_ready = sem("tanh_ready")
        us_ready = sem("us_ready")
        ag_ready = sem("ag_ready")
        q_ready = sem("q_ready")
        hid_ready = sem("hid_ready")
        down_done = sem("down_done")
        y_final = sem("y_final")

        TURNED, FULL = (0, HT), (0, HT)
        LOW, SMALL, RAWB = (GB, HT), (UB, ACC + 1), (ACC, ACC)
        hT = ps[:, HT:HT + 2, :].rearrange("p a (j d) -> p (a j) d", d=H)
        acc = ps[:, ACC:ACC + 2, :].rearrange("p a (j d) -> p (a j) d", d=H)

        def tiles(b):
            return slice(TB * b, TB * b + TB)

        def tokens(b):
            return slice(L * b, L * b + L)

        def state(b, n0, i):
            return N * b + n0 + 2 * i

        def chunk(b, n0, i):
            return (N + 1) * b + n0 + 2 * i

        def chunk_slot(b, n0):
            return ((N + 1) * b + n0) % 2

        def chunk_use(b, n0, i):
            return ((N + 1) * b + n0) // 2 + i + 1

        def after(b, n0):
            return (b, n0 + 1) if n0 < N else (b + 1, 0)

        def rows_of(n0):
            return P if n0 < N else TAIL

        def steps(eng, b, step, between=lambda b, n0: None):
            for n0 in range(2):
                step(b, n0, 0)
                between(b, n0)
            with eng.Fori(0, N // 2 - 2) as i:
                step(b, 2, i)
                step(b, 3, i)
            for n0 in range(N - 2, N + 1):
                step(b, n0, 0)
                between(b, n0)

        block = ctx.enter_context(nc.Block())

        @block.sync
        def _(sp):
            xv = x.rearrange("(t p) d -> p t d", p=P)
            ov = out.rearrange("(t p) d -> p t d", p=P)
            sp.dma_start(xt[:, tiles(0), :], xv[:, tiles(0), :]).then_inc(x_in[0], 16)
            sp.dma_start(con[:, :], consts).then_inc(con_in, 16)
            sp.dma_start(wdel_s[:, :, :], wdel).then_inc(wdel_in, 16)
            sp.dma_start(wsm_s[:, :, :], wsm).then_inc(wsm_in, 16)
            sp.dma_start(wb_s[:, :, :], wb).then_inc(wb_in, 16)
            sp.dma_start(wdt_s[:, :, :], wdt).then_inc(wdt_in, 16)

            def load_gate_up(b, n0, i):
                m, slot = chunk(b, n0, i), chunk_slot(b, n0)
                if b == 0 and n0 in (2, 3):
                    sp.wait_ge(wl_first[slot], 1)
                elif not (b == 0 and n0 < 2):
                    sp.wait_ge(wl_ready, m - 3)
                if n0 == N:
                    sp.dma_start(wg_r[:, slot, :, :, 0:TAIL], wgu_tail).then_inc(wg_in[slot], 16)
                else:
                    src = wgu[bass.ds(n0 + 2 * i, 1)].rearrange("a p g k f -> (a p) g k f")
                    sp.dma_start(wg_r[:, slot, :, :, :], src).then_inc(wg_in[slot], 16)

            def load_down(b, n0, i):
                m, slot = chunk(b, n0, i), chunk_slot(b, n0)
                if not (b == 0 and n0 < 2):
                    sp.wait_ge(down_done, m - 1)
                if n0 == N:
                    sp.dma_start(wd_r[0:TAIL, slot, :], wd[N * P:F, :]).then_inc(wd_in[slot], 16)
                else:
                    sp.dma_start(wd_r[:, slot, :], wd[bass.ds((n0 + 2 * i) * P, P), :]).then_inc(wd_in[slot], 16)

            def store(b):
                for k in range(2):
                    t = slice(TB * b + 2 * k, TB * b + 2 * k + 2)
                    sp.wait_ge(y_final, 2 * b + k + 1)
                    sp.dma_start(ov[:, t, :], yacc[:, t, :]).then_inc(stored, 16)

            load_gate_up(0, 0, 0)
            sp.dma_start(xt[:, tiles(1), :], xv[:, tiles(1), :]).then_inc(x_in[1], 16)
            for b in range(NB):
                for n0 in range(4):
                    if (b, n0) != (0, 0):
                        load_gate_up(b, n0, 0)
                    if n0 > 0:
                        load_down(b, n0 - 1, 0)
                    elif b:
                        load_down(b - 1, N, 0)
                with sp.Fori(0, N // 2 - 2) as i:
                    for n0 in (4, 5):
                        load_gate_up(b, n0, i)
                        load_down(b, n0 - 1, i)
                load_gate_up(b, N, 0)
                load_down(b, N - 1, 0)
            load_down(NB - 1, N, 0)
            for b in range(NB):
                store(b)
            sp.wait_ge(stored, 16 * 2 * NB)

        @block.gpsimd
        def _(pool):
            chain = [0]

            def link(ins):
                chain[0] += 1
                ins.then_inc(pool_chain, 1)
                pool.wait_ge(pool_chain, chain[0])

            def low_x(b):
                c = tokens(b)
                pool.wait_ge(xh_ready, b + 1)
                pool.tensor_tensor(xl[:, :, c], xnT[:, :, c], xh[:, :, c].bitcast(F32), ALU.subtract)\
                    .then_inc(xl_ready, 1)

            def low_w(n0):
                pool.wait_ge(wh_ready, n0 + 1)
                pool.tensor_tensor(wg_l[:, n0, :, :, :], wg_r[:, n0, :, :, :],
                                   wg_h[:, n0, :, :, :].bitcast(F32), ALU.subtract).then_inc(wl_first[n0], 1)

            def drift(b):
                c = tokens(b)
                pool.wait_ge(delta_ready, b + 1)
                pool.tensor_tensor(u[:, :, c], delta[:, :, c], xnT[:, :, c], ALU.mult).then_inc(u_written[b], 1)

            def drive(b, n0, i):
                s = state(b, n0, i)
                slot = n0 % 2
                pool.wait_ge(b_copied, s + 1)
                if not (b == 0 and n0 < 2):
                    pool.wait_ge(scanned, KC * (s - 1))
                if n0 == 0:
                    pool.wait_ge(u_written[b], 1)
                bs = bb[:, slot, :]
                pool.tensor_tensor(bx[:, slot, :, :], u[:, :, tokens(b)],
                                   bs[:, None, :].to_broadcast([P, KC, L]), ALU.mult).then_inc(bx_ready, 1)

            def weigh(b, n0, i):
                m, slot, r = chunk(b, n0, i), chunk_slot(b, n0), rows_of(n0)
                pool.wait_ge(us_ready, m + 1)
                pool.wait_ge(c_copied, m + 1)
                pool.tensor_tensor(us[0:r, slot, :], us[0:r, slot, :], cb[0:r, slot, :], ALU.mult)\
                    .then_inc(q_ready, 1)

            def hidden(b, n0, i):
                m, slot, r = chunk(b, n0, i), chunk_slot(b, n0), rows_of(n0)
                pool.wait_ge(q_ready, m + 1)
                pool.wait_ge(ag_ready, m + 1)
                if not (b == 0 and n0 < 2):
                    pool.wait_ge(down_done, m - 1)
                pool.tensor_tensor(hid[0:r, slot, :], ag[0:r, slot, :], us[0:r, slot, :], ALU.mult)\
                    .then_inc(hid_ready, 1)

            def step(b, n0, i):
                nb, nn = after(b, n0)
                weigh(b, n0, i)
                if nn < N and nb < NB:
                    drive(nb, nn, i)
                hidden(b, n0, i)

            def between(b, n0):
                if b + 1 < NB and n0 == 1:
                    low_x(b + 1)
                if b + 1 < NB and n0 == N - 2:
                    drift(b + 1)

            def cut_b():
                r, s = raw[:, 0, 0, :], stack[:, 0, 0, :]
                link(pool.tensor_copy(s, r))
                link(pool.tensor_tensor(rest_b[:, :], r, s, ALU.subtract))
                link(pool.tensor_copy(mid_b[:, :], rest_b[:, :]))
                link(pool.tensor_copy(s[STP:2 * STP, :], mid_b[STP:2 * STP, :]))
                pool.tensor_tensor(s[2 * STP:SK, :], rest_b[2 * STP:SK, :], mid_b[2 * STP:SK, :], ALU.subtract)\
                    .then_inc(stack_b, 1)
                pool.wait_ge(stack_b, 1)

            pool.memset(warm[:, :], 0.0).then_inc(warm_ready, 1)
            pool.memset(zt[:, :, :, :], 0.0).then_inc(zt_zero, 1)
            low_w(0)
            low_x(0)
            pool.wait_ge(rb_ready, 1)
            cut_b()
            low_w(1)
            drive(0, 0, 0)
            for b in range(NB):
                steps(pool, b, step, between)

        @block.scalar
        def _(act):
            act.dma_start(A[:, :], alog).then_inc(alog_in, 16)
            act.dma_start(bdt_s[:, :], bdt).then_inc(bdt_in, 16)
            act.dma_start(dsk_s[:, :], dskip).then_inc(dsk_in, 16)
            def root(b):
                act.wait_ge(ve_ready, b + 1)
                act.activation(sd[:, tiles(b)], ve[:, tiles(b)], ACT.Sqrt).then_inc(sd_ready, 1)

            def normalise(b):
                act.wait_ge(nm_ready, b + 1)
                for t in range(TB * b + 2, TB * b + 4):
                    act.activation(xn[:, t, :], xt[:, t, :], ACT.Identity, bias=nm[:, t:t + 1], scale=rs[:, t:t + 1])\
                       .then_inc(xn_act, 1)

            def turned_x(b):
                act.wait_ge(xnT_ps, b + 1)
                act.activation(xnT[:, 1, tokens(b)], ps[:, TURNED[b] + 1, :], ACT.Copy).then_inc(xnT_ready[1], 1)

            def low_rank(b):
                act.wait_ge(dtr_ps, b + 1)
                act.activation(dtr[:, b, :], ps[0:R, LOW[b], :], ACT.Copy).then_inc(dtr_ready, 1)

            def high_x(b):
                for kc in range(KC):
                    act.wait_ge(xnT_ready[kc], b + 1)
                act.activation(xh[:, :, tokens(b)], xnT[:, :, tokens(b)], ACT.Copy).then_inc(xh_ready, 1)

            def raw_b(b):
                act.wait_ge(rb_ps, b + 1)
                act.activation(raw[:, b, 0, :], ps[0:SK, RAWB[b], :], ACT.Copy).then_inc(rb_ready, 1)

            def raw_c(b, bank):
                act.wait_ge(zt_ps, b + 1)
                act.activation(raw[:, b, 1, :], ps[0:SK, bank, :], ACT.Copy).then_inc(rc_ready, 1)

            def high_w(b, n0, i):
                m, slot = chunk(b, n0, i), chunk_slot(b, n0)
                w = slice(0, rows_of(n0))
                act.wait_ge(wg_in[slot], 16 * chunk_use(b, n0, i))
                if not (b == 0 and n0 < 2):
                    act.wait_ge(g_ready, m - 1)
                act.activation(wg_h[:, slot, :, :, w], wg_r[:, slot, :, :, w], ACT.Copy).then_inc(wh_ready, 1)

            def soft_abs(b):
                act.wait_ge(z_ps, b + 1)
                for kc in range(KC):
                    act.activation(soft[:, kc, tokens(b)], ps[:, FULL[b] + kc, :], ACT.Abs,
                                   bias=bdt_s[:, kc:kc + 1]).then_inc(z_abs, 1)

            def soft_exp(b):
                c = soft[:, :, tokens(b)]
                act.wait_ge(z_abs, KC * (b + 1))
                act.activation(c, c, ACT.Exp, scale=-1.0).then_inc(act_chain, 1)

            def soft_log(b):
                c = soft[:, :, tokens(b)]
                act.wait_ge(act_chain, b + 1)
                act.activation(c, c, ACT.Ln, bias=1.0).then_inc(soft_ready, 1)

            def router_exp(b):
                act.wait_ge(lg_ready, b + 1)
                act.activation(eg[:, tiles(b), :], lg[:, tiles(b), :], ACT.Exp).then_inc(eg_ready, 1)

            def b_copy(b, n0, i):
                s = state(b, n0, i)
                act.wait_ge(b_ps, s + 1)
                if not (b == 0 and n0 < 2):
                    act.wait_ge(bx_ready, s - 1)
                act.activation(bb[:, n0 % 2, :], ps[:, UB, :], ACT.Copy).then_inc(b_copied, 1)

            def decay(b, n0, i, kc):
                s = state(b, n0, i)
                if n0 == 0:
                    act.wait_ge(delta_ready, b + 1)
                if b == 0 and n0 == 0:
                    act.wait_ge(A_ready, 1)
                else:
                    act.wait_ge(scanned, KC * (s - 1) + kc + 1)
                n = n0 + 2 * i
                act.activation(ps[:, DA + kc, :], delta[:, kc, tokens(b)], ACT.Exp,
                               scale=A[:, bass.ds(kc * N + n, 1)]).then_inc(dA_ready, 1)

            def c_copy(b, n0, i):
                m, slot, r = chunk(b, n0, i), chunk_slot(b, n0), rows_of(n0)
                act.wait_ge(c_ps, m + 1)
                if not (b == 0 and n0 < 2):
                    act.wait_ge(q_ready, m - 1)
                act.activation(cb[0:r, slot, :], ps[0:r, UB, :], ACT.Copy).then_inc(c_copied, 1)

            def halve_up(b, n0, i):
                m, slot, r = chunk(b, n0, i), chunk_slot(b, n0), rows_of(n0)
                act.wait_ge(u_ready, m + 1)
                if not (b == 0 and n0 < 2):
                    act.wait_ge(hid_ready, m - 1)
                act.activation(us[0:r, slot, :], ps[0:r, UB, :], ACT.Copy, scale=0.5).then_inc(us_ready, 1)

            def tanh(b, n0, i):
                m, slot, r = chunk(b, n0, i), chunk_slot(b, n0), rows_of(n0)
                act.wait_ge(g_ready, m + 1)
                if not (b == 0 and n0 < 2):
                    act.wait_ge(ag_ready, m - 1)
                act.activation(th[0:r, slot, :], ps[0:r, GB, :], ACT.Tanh, scale=0.5).then_inc(tanh_ready, 1)

            def step(b, n0, i):
                nb, nn = after(b, n0)
                scans = nn < N and nb < NB
                if b == 0 and n0 == 0:
                    b_copy(nb, nn, i)
                    c_copy(b, n0, i)
                    for kc in range(KC):
                        decay(nb, nn, i, kc)
                    c_copy(nb, nn, i)
                    return
                if nb < NB:
                    high_w(nb, nn, i)
                halve_up(b, n0, i)
                if scans:
                    decay(nb, nn, i, 0)
                tanh(b, n0, i)
                if scans:
                    b_copy(nb, nn, i)
                    decay(nb, nn, i, 1)
                if nb < NB:
                    c_copy(nb, nn, i)

            def between(b, n0):
                if b + 1 < NB and n0 == 1:
                    router_exp(b + 1)
                if b + 1 < NB and n0 == N - 2:
                    soft_log(b + 1)
                    raw_c(b + 1, GB)

            root(0)
            high_w(0, 0, 0)
            normalise(0)
            root(1)
            turned_x(0)
            high_x(0)
            high_w(0, 1, 0)
            act.dma_start(sel[:, :], selectors).then_inc(sel_in, 16)
            raw_b(0)
            act.wait_ge(alog_in, 16)
            act.activation(A[:, :], A[:, :], ACT.Exp).then_inc(A_exp, 1)
            router_exp(0)
            act.wait_ge(bdt_in, 16)
            soft_abs(0)
            soft_exp(0)
            soft_log(0)
            normalise(1)
            halve_up(0, 0, 0)
            tanh(0, 0, 0)
            turned_x(1)
            b_copy(0, 0, 0)
            for kc in range(KC):
                decay(0, 0, 0, kc)
            raw_c(0, ACC)
            low_rank(1)
            raw_b(1)
            high_x(1)
            soft_abs(1)
            soft_exp(1)
            for b in range(NB):
                steps(act, b, step, between)

        @block.vector
        def _(dve):
            chain = [0]

            def link(ins):
                chain[0] += 1
                ins.then_inc(dve_chain, 1)
                dve.wait_ge(dve_chain, chain[0])

            def moments(b):
                t = tiles(b)
                dve.wait_ge(x_in[b], 16)
                for k in range(TB * b, TB * b + TB):
                    last = dve.bn_stats(stats[:, k, :], xt[:, k, :])
                link(last)
                for k in range(TB * b, TB * b + TB):
                    last = dve.bn_aggr(mv[:, k, :], stats[:, k, :])
                link(last)
                dve.tensor_scalar(ve[:, t], mv[:, t, 1], EPS, None, ALU.add).then_inc(ve_ready, 1)

            def roots(b):
                t = tiles(b)
                dve.wait_ge(sd_ready, b + 1)
                link(dve.reciprocal(rs[:, t], sd[:, t]))
                link(dve.tensor_tensor(rt[:, t], rs[:, t], rs[:, t], ALU.mult))
                link(dve.tensor_tensor(rt[:, t], rt[:, t], ve[:, t], ALU.mult))
                link(dve.tensor_scalar(rt[:, t], rt[:, t], -0.5, 1.5, ALU.mult, ALU.add))
                link(dve.tensor_tensor(rs[:, t], rs[:, t], rt[:, t], ALU.mult))
                dve.scalar_tensor_tensor(nm[:, t], mv[:, t, 0], -1.0, rs[:, t], ALU.mult, ALU.mult)\
                   .then_inc(nm_ready, 1)

            def normalise(b):
                for k in range(TB * b, TB * b + 2):
                    dve.tensor_scalar(xn[:, k, :], xt[:, k, :], mv[:, k, 0:1], rs[:, k:k + 1],
                                      ALU.subtract, ALU.mult).then_inc(xn_dve, 1)

            def turned_x(b):
                dve.wait_ge(xnT_ps, b + 1)
                dve.tensor_copy(xnT[:, 0, tokens(b)], ps[:, TURNED[b], :]).then_inc(xnT_ready[0], 1)

            def cut(b, which, done):
                r, s = raw[:, b, which, :], stack[:, b, which, :]
                link(dve.tensor_copy(s, r))
                link(dve.tensor_tensor(rest[:, :], r, s, ALU.subtract))
                link(dve.tensor_copy(mid[:, :], rest[:, :]))
                dve.tensor_copy(s[STP:2 * STP, :], mid[STP:2 * STP, :])
                dve.tensor_tensor(s[2 * STP:SK, :], rest[2 * STP:SK, :], mid[2 * STP:SK, :], ALU.subtract)\
                   .then_inc(done, 1)
                dve.wait_ge(done, b + 1)

            def positive(b):
                for kc in range(KC):
                    dve.wait_ge(z_abs, KC * b + kc + 1)
                    dve.tensor_scalar(delta[:, kc, tokens(b)], ps[:, FULL[b] + kc, :], bdt_s[:, kc:kc + 1], 0.0,
                                      ALU.add, ALU.max).then_inc(z_pos, 1)

            def make_delta(b):
                c = tokens(b)
                dve.wait_ge(soft_ready, b + 1)
                dve.wait_ge(z_pos, KC * (b + 1))
                dve.tensor_tensor(delta[:, :, c], delta[:, :, c], soft[:, :, c], ALU.add).then_inc(delta_ready, 1)

            def logits(b):
                t = tiles(b)
                dve.wait_ge(sm_ps, TB * (b + 1))
                dve.tensor_copy(sm[:, t, :], ps[:, SMALL[b], 0:TB * SMP]
                                .rearrange("p (t c) -> p t c", c=SMP)[:, :, 0:SM]).then_inc(sm_copied, 1)
                dve.wait_ge(sm_copied, b + 1)
                link(dve.tensor_reduce(rmx[:, t], sm[:, t, SM_R:SM_R + E], AX.X, ALU.max))
                dve.tensor_tensor(lg[:, t, 0:E], sm[:, t, SM_R:SM_R + E], rmx[:, t, None].to_broadcast([P, TB, E]),
                                  ALU.subtract)
                dve.tensor_scalar(lg[:, t, E], sm[:, t, SM_G], -1.0, 80.0, ALU.mult, ALU.min).then_inc(lg_ready, 1)

            def route(b):
                t = tiles(b)
                dve.wait_ge(eg_ready, b + 1)
                dve.tensor_reduce(rsum[:, t, 0], eg[:, t, 0:E], AX.X, ALU.add)
                link(dve.tensor_scalar(rsum[:, t, 1], eg[:, t, E], 1.0, None, ALU.add))
                link(dve.reciprocal(rsum[:, t, :], rsum[:, t, :]))
                dve.tensor_copy(zt[:, t, :, 0], rsum[:, t, 1:2].to_broadcast([P, TB, PARTS]))
                link(dve.tensor_tensor(pr[:, t, :], eg[:, t, 0:E], rsum[:, t, 0:1].to_broadcast([P, TB, E]),
                                       ALU.mult))
                other = pr[:, t, None, :].to_broadcast([P, TB, E, E])
                own = pr[:, t, :, None].to_broadcast([P, TB, E, E])
                dve.tensor_tensor(beats[:, :, :, :], other, own, ALU.is_gt)
                link(dve.tensor_tensor(ties[:, :, :, :], other, own, ALU.is_equal))
                link(dve.tensor_tensor(ties[:, :, :, :], ties[:, :, :, :],
                                       lower[:, None, :, :].to_broadcast([P, TB, E, E]), ALU.mult))
                link(dve.tensor_tensor(beats[:, :, :, :], beats[:, :, :, :], ties[:, :, :, :], ALU.add))
                link(dve.tensor_reduce(rank[:, :, :], beats[:, :, :, :], AX.X, ALU.add))
                link(dve.scalar_tensor_tensor(pr[:, t, :], rank[:, :, :], float(TOPK), pr[:, t, :],
                                              ALU.is_lt, ALU.mult))
                dve.tensor_copy(zt[:, t, :, 1:1 + E], pr[:, t, None, :].to_broadcast([P, TB, PARTS, E]))\
                   .then_inc(zt_ready, 1)

            def low_w(b, n0, i):
                m, slot = chunk(b, n0, i), chunk_slot(b, n0)
                w = slice(0, rows_of(n0))
                dve.wait_ge(wh_ready, m + 1)
                dve.tensor_tensor(wg_l[:, slot, :, :, w], wg_r[:, slot, :, :, w],
                                  wg_h[:, slot, :, :, w].bitcast(F32), ALU.subtract).then_inc(wl_ready, 1)

            def scan(b, n0, i):
                s, slot = state(b, n0, i), n0 % 2
                dve.wait_ge(bx_ready, s + 1)
                if not (b == 0 and n0 < 2):
                    dve.wait_ge(hT_ready, s - 1)
                for kc in range(KC):
                    dve.wait_ge(dA_ready, KC * s + kc + 1)
                    dve.tensor_tensor_scan(h[:, slot, kc, :], ps[:, DA + kc, :], bx[:, slot, kc, :], 0.0,
                                           ALU.mult, ALU.add).then_inc(scanned, 1)

            def add_y(b, n0, i):
                s = state(b, n0, i)
                n = n0 + 2 * i
                dve.wait_ge(hT_ready, s + 1)
                if n0 > 0:
                    dve.wait_ge(y_added, s)
                before = xt if n0 == 0 else yacc
                for j in range(TB):
                    t = TB * b + j
                    last = dve.scalar_tensor_tensor(yacc[:, t, :], hT[:, j, :], sm[:, t, bass.ds(SM_C + n, 1)],
                                                    before[:, t, :], ALU.mult, ALU.add)
                last.then_inc(y_added, 1)

            def silu(b, n0, i):
                m, slot, r = chunk(b, n0, i), chunk_slot(b, n0), rows_of(n0)
                dve.wait_ge(tanh_ready, m + 1)
                if not (b == 0 and n0 < 2):
                    dve.wait_ge(hid_ready, m - 1)
                dve.scalar_tensor_tensor(ag[0:r, slot, :], th[0:r, slot, :], 1.0, ps[0:r, GB, :],
                                         ALU.add, ALU.mult).then_inc(ag_ready, 1)

            def finish(b):
                dve.wait_ge(y_added, N * (b + 1))
                dve.wait_ge(down_done, (N + 1) * (b + 1))
                for k in range(2):
                    t = slice(TB * b + 2 * k, TB * b + 2 * k + 2)
                    dve.tensor_tensor(yacc[:, t, :], yacc[:, t, :], acc[:, 2 * k:2 * k + 2, :], ALU.add)\
                       .then_inc(y_final, 1)

            def step(b, n0, i):
                nb, nn = after(b, n0)
                if n0 < N:
                    scan(b, n0, i)
                if b == 0 and n0 == 0:
                    return
                if n0 > 0:
                    add_y(b, n0 - 1, i)
                if nb < NB:
                    low_w(nb, nn, i)
                silu(b, n0, i)

            def between(b, n0):
                if b and n0 == 0:
                    finish(b - 1)
                if b + 1 < NB and n0 == N - 2:
                    dve.wait_ge(rb_ready, b + 2)
                    cut(b + 1, 0, stack_b)
                    route(b + 1)
                    make_delta(b + 1)
                if b + 1 < NB and n0 == N - 1:
                    dve.wait_ge(rc_ready, b + 2)
                    cut(b + 1, 1, stack_c)

            moments(0)
            roots(0)
            normalise(0)
            moments(1)
            turned_x(0)
            dve.wait_ge(dtr_ps, 1)
            dve.tensor_copy(dtr[:, 0, :], ps[0:R, LOW[0], :]).then_inc(dtr_first, 1)
            logits(0)
            roots(1)
            normalise(1)
            dve.wait_ge(A_exp, 1)
            dve.tensor_scalar(A[:, :], A[:, :], -1.0, None, ALU.mult).then_inc(A_ready, 1)
            dve.wait_ge(zt_zero, 1)
            dve.wait_ge(con_in, 16)
            route(0)
            dve.wait_ge(bdt_in, 16)
            positive(0)
            make_delta(0)
            dve.wait_ge(delta_ready, 1)
            dve.tensor_tensor(u[:, :, tokens(0)], delta[:, :, tokens(0)], xnT[:, :, tokens(0)], ALU.mult)\
               .then_inc(u_written[0], 1)
            turned_x(1)
            silu(0, 0, 0)
            dve.wait_ge(rc_ready, 1)
            cut(0, 1, stack_c)
            logits(1)
            positive(1)
            dve.wait_ge(dsk_in, 16)
            for kc in range(KC):
                last = dve.tensor_scalar(dd[:, kc, :], ident, dsk_s[:, kc:kc + 1], None, ALU.mult)
            last.then_inc(dd_ready, 1)
            for b in range(NB):
                steps(dve, b, step, between)
            finish(NB - 1)

        @block.tensor
        def _(pe):
            def turn_x(b):
                for j in range(TB):
                    if j < 2:
                        pe.wait_ge(xn_dve, 2 * b + j + 1)
                    else:
                        pe.wait_ge(xn_act, 2 * b + j - 1)
                    for kc in range(KC):
                        last = pe.transpose(ps[:, TURNED[b] + kc, j * P:(j + 1) * P],
                                            xn[:, TB * b + j, kc * P:(kc + 1) * P], ident)
                last.then_inc(xnT_ps, 1)

            def low_rank(b):
                for kc in range(KC):
                    pe.wait_ge(xnT_ready[kc], b + 1)
                    last = pe.matmul(ps[0:R, LOW[b], :], wdel_s[:, kc, :], xnT[:, kc, tokens(b)],
                                     start=kc == 0, stop=kc == KC - 1)
                last.then_inc(dtr_ps, 1)

            def raw_b(b):
                if b:
                    pe.wait_ge(rb_ready, b)
                for kc in range(KC):
                    last = pe.matmul(ps[0:SK, RAWB[b], :], wb_s[:, kc, :], xnT[:, kc, tokens(b)],
                                     start=kc == 0, stop=kc == KC - 1)
                last.then_inc(rb_ps, 1)

            def full_rank(b):
                pe.wait_ge(dtr_ready if b else dtr_first, 1)
                for kc in range(KC):
                    last = pe.matmul(ps[:, FULL[b] + kc, :], wdt_s[:, kc, :], dtr[:, b, :], start=True, stop=True)
                last.then_inc(z_ps, 1)

            def small(b):
                for j in range(TB):
                    t = TB * b + j
                    for kc in range(KC):
                        last = pe.matmul(ps[:, SMALL[b], SMP * j:SMP * j + SM], xnT[:, kc, t * P:(t + 1) * P],
                                         wsm_s[:, kc, :], start=kc == 0, stop=kc == KC - 1)
                    last.then_inc(sm_ps, 1)

            def turn_weights(b, bank):
                pe.wait_ge(zt_ready, b + 1)
                for j in range(TB):
                    last = pe.transpose(ps[0:SK, bank, j * P:(j + 1) * P],
                                        zt[:, TB * b + j, :, :].rearrange("p a c -> p (a c)"), ident)
                last.then_inc(zt_ps, 1)

            def spread_b(b, n0, i):
                n = n0 + 2 * i
                if n0 == 0:
                    pe.wait_ge(stack_b, b + 1)
                pe.matmul(ps[:, UB, :], sel[:, bass.ds(n * P, P)], stack[:, b, 0, :],
                          start=True, stop=True).then_inc(b_ps, 1)

            def spread_c(b, n0, i):
                n, r = n0 + 2 * i, rows_of(n0)
                if n0 == 0:
                    pe.wait_ge(stack_c, b + 1)
                pe.matmul(ps[0:r, UB, :], sel[:, bass.ds(N * P + n * P, r)], stack[:, b, 1, :],
                          start=True, stop=True).then_inc(c_ps, 1)

            def turn_h(b, n0, i):
                s, slot = state(b, n0, i), n0 % 2
                pe.wait_ge(scanned, KC * (s + 1))
                if b == 0 and n0 == 0:
                    pe.wait_ge(z_pos, KC * NB)
                else:
                    pe.wait_ge(y_added, s)
                for j in range(TB):
                    for kc in range(KC):
                        last = pe.transpose(hT[:, j, kc * P:(kc + 1) * P], h[:, slot, kc, j * P:(j + 1) * P], ident)
                last.then_inc(hT_ready, 1)

            def project(b, n0, which):
                slot = chunk_slot(b, n0)
                bank, done = ((GB, g_ready), (UB, u_ready))[which]
                c = tokens(b)
                for kc in range(KC):
                    for k, (w, xs) in enumerate(((wg_h, xh), (wg_h, xl), (wg_l, xh))):
                        last = pe.matmul(ps[:, bank, :], w[:, slot, which, kc, :], xs[:, kc, c],
                                         start=kc == 0 and k == 0, stop=kc == KC - 1 and k == 2)
                last.then_inc(done, 1)

            def skip(b):
                if b:
                    pe.wait_ge(y_final, 2 * b)
                else:
                    pe.wait_ge(dd_ready, 1)
                    pe.wait_ge(rb_ready, NB)
                    pe.wait_ge(rc_ready, 1)
                    pe.wait_ge(sm_copied, NB)
                for j in range(TB):
                    for kc in range(KC):
                        pe.matmul(acc[:, j, kc * P:(kc + 1) * P], xnT[:, kc, (TB * b + j) * P:(TB * b + j + 1) * P],
                                  dd[:, kc, :], start=kc == 0 and j % 2 == 0, stop=True, skip_group_check=True)

            def down(b, n0, i):
                m, slot, r = chunk(b, n0, i), chunk_slot(b, n0), rows_of(n0)
                pe.wait_ge(hid_ready, m + 1)
                pe.wait_ge(wd_in[slot], 16 * chunk_use(b, n0, i))
                for j in range(TB):
                    last = pe.matmul(acc[:, j, :], hid[0:r, slot, j * P:(j + 1) * P], wd_r[0:r, slot, :],
                                     start=False, stop=True, skip_group_check=True)
                last.then_inc(down_done, 1)

            def up_gate(b, n0, i):
                m, slot = chunk(b, n0, i), chunk_slot(b, n0)
                if n0 == 0:
                    pe.wait_ge(xl_ready, b + 1)
                if b == 0 and n0 < 2:
                    pe.wait_ge(wl_first[slot], 1)
                else:
                    pe.wait_ge(wl_ready, m - 1)
                project(b, n0, 1)
                if not (b == 0 and n0 == 0):
                    pe.wait_ge(ag_ready, m)
                project(b, n0, 0)

            def step(b, n0, i):
                m = chunk(b, n0, i)
                nb, nn = after(b, n0)
                scans = nn < N and nb < NB
                if not (b == 0 and n0 == 0):
                    pe.wait_ge(c_copied, m + 1)
                    up_gate(b, n0, i)
                    pe.wait_ge(us_ready, m + 1)
                    if scans:
                        spread_b(nb, nn, i)
                    if n0 > 0:
                        if b and n0 == 1:
                            skip(b)
                        down(b, n0 - 1, i)
                    else:
                        down(b - 1, N, 0)
                    if nb < NB:
                        if scans:
                            pe.wait_ge(b_copied, state(nb, nn, i) + 1)
                        spread_c(nb, nn, i)
                if n0 < N:
                    turn_h(b, n0, i)

            def between(b, n0):
                if b + 1 < NB and n0 == N - 2:
                    pe.wait_ge(ag_ready, chunk(b, n0, 0) + 1)
                    turn_weights(b + 1, GB)
                    pe.wait_ge(rc_ready, b + 2)

            def wake(count):
                for k in range(count):
                    pe.matmul(ps[:, ACC + 1, :], warm[:, 0:P], warm[:, :], start=True, stop=True)

            pe.wait_ge(warm_ready, 1)
            wake(WARM)
            pe.wait_ge(con_in, 16)
            turn_x(0)
            wake(3)
            pe.wait_ge(wdel_in, 16)
            low_rank(0)
            pe.wait_ge(wsm_in, 16)
            small(0)
            pe.wait_ge(wb_in, 16)
            raw_b(0)
            pe.wait_ge(wdt_in, 16)
            full_rank(0)
            pe.wait_ge(sm_copied, 1)
            up_gate(0, 0, 0)
            turn_x(1)
            pe.wait_ge(sel_in, 16)
            pe.wait_ge(us_ready, 1)
            spread_b(0, 0, 0)
            turn_weights(0, ACC)
            low_rank(1)
            small(1)
            pe.wait_ge(b_copied, 1)
            spread_b(0, 1, 0)
            pe.wait_ge(rc_ready, 1)
            raw_b(1)
            full_rank(1)
            pe.wait_ge(b_copied, 2)
            spread_c(0, 0, 0)
            pe.wait_ge(c_copied, 1)
            spread_c(0, 1, 0)
            skip(0)
            for b in range(NB):
                steps(pe, b, step, between)
            down(NB - 1, N, 0)


def kernel(L0_attn_x, L0_attn_W_xproj, L0_attn_W_dt, L0_attn_b_dt, L0_attn_A_log, L0_attn_D, L0_ffn_Wr,
           L0_ffn_Wg, L0_ffn_Wu, L0_ffn_Wd, L0_ffn_Sg, L0_ffn_Su, L0_ffn_Sd, L0_ffn_Wsg):
    import ml_dtypes
    import numpy as np
    import concourse.bacc as bacc
    from concourse.bass_utils import run_bass_kernel_spmd

    def f(a):
        return np.asarray(a)

    wx = f(L0_attn_W_xproj)
    gate = np.concatenate([f(L0_ffn_Sg), f(L0_ffn_Wg).transpose(1, 0, 2).reshape(H, E * FE)], axis=1)
    up = np.concatenate([f(L0_ffn_Su), f(L0_ffn_Wu).transpose(1, 0, 2).reshape(H, E * FE)], axis=1)
    gu = np.stack([gate, up]).reshape(2, KC, P, F).transpose(2, 0, 1, 3)
    consts = np.concatenate([np.eye(P, dtype=np.float32),
                             np.tile(np.tril(np.ones((E, E), np.float32), -1).reshape(1, E * E), (P, 1))], axis=1)
    unit = np.arange(F)
    owner = np.where(unit < FS, 0, 1 + (unit - FS) // FE)
    picked = np.concatenate([np.repeat(np.arange(N), P), owner])
    selectors = (np.arange(SK)[:, None] % STP == picked[None, :]).astype(ml_dtypes.bfloat16)

    arrays = {
        "x": f(L0_attn_x).reshape(NB * L, H),
        "wgu": gu[..., :N * P].reshape(P, 2, KC, N, P).transpose(3, 0, 1, 2, 4),
        "wgu_tail": gu[..., N * P:],
        "wd": np.concatenate([f(L0_ffn_Sd), f(L0_ffn_Wd).reshape(E * FE, H)], axis=0),
        "wsm": np.concatenate([f(L0_ffn_Wr), f(L0_ffn_Wsg), wx[R + N:].T], axis=1).reshape(KC, P, SM).transpose(1, 0, 2),
        "wdel": wx[:R].T.reshape(KC, P, R).transpose(1, 0, 2),
        "wb": np.tile(wx[R:], (PARTS, 1)).T.reshape(KC, P, SK).transpose(1, 0, 2),
        "wdt": f(L0_attn_W_dt).T.reshape(R, KC, P),
        "bdt": f(L0_attn_b_dt).reshape(KC, P).T,
        "alog": f(L0_attn_A_log).reshape(KC, P, N).transpose(1, 0, 2).reshape(P, KC * N),
        "dskip": f(L0_attn_D).reshape(KC, P).T,
        "consts": consts,
        "selectors": selectors,
    }
    arrays = {k: np.ascontiguousarray(v) for k, v in arrays.items()}
    nc = bacc.Bacc("TRN2", target_bir_lowering=False, num_devices=1)
    args = {k: nc.dram_tensor(k, v.shape, mybir.dt.from_np(v.dtype), kind="ExternalInput").ap()
            for k, v in arrays.items()}
    args["out"] = nc.dram_tensor("out", (NB * L, H), F32, kind="ExternalOutput").ap()
    build(nc, **args)
    r = run_bass_kernel_spmd(nc, [arrays], core_ids=[0])
    return r.results[0]["out"].reshape(NB, L, H)
```

```python
from contextlib import ExitStack

import concourse.bass as bass
from concourse import mybir

ALU = mybir.AluOpType
ACT = mybir.ActivationFunctionType
AX = mybir.AxisListType
F32 = mybir.dt.float32
F32R = mybir.dt.float32r
BF16 = mybir.dt.bfloat16

P = 128
NB = 2
L = 512
H = 256
KC = H // P
TB = L // P
NT = NB * TB
R = 64
N = 16
E = 8
FE = 176
FS = 704
F = FS + E * FE
TAIL = F - N * P
TOPK = 2
EPS = 1e-5

SM_R, SM_G, SM_C, SM_B, SM = 0, E, E + 1, E + 1 + N, E + 1 + 2 * N
PR = R + 1 + SM
PARTS, STP = 3, 32
ROW_B, ROWS = 1 + E, 1 + E + N
SK = PARTS * STP
WARM = 16

DA, HT, GB, UB, ACC = 0, 2, 4, 5, 6


def build(nc, x, wgu, wgu_tail, wd, wproj, wdt, alog, dskip, consts, selectors, out):
    ctx = ExitStack()
    with ctx:
        def sb(name, shape, dt=F32):
            return ctx.enter_context(nc.sbuf_tensor(name, shape, dt))

        def sem(name):
            return ctx.enter_context(nc.semaphore(name))

        def sems(name, n):
            return [sem(f"{name}{k}") for k in range(n)]

        ps = ctx.enter_context(nc.psum_tensor("ps", [P, 8, 512], F32))

        xt = sb("xt", [P, NT, H])
        xn = sb("xn", [P, NT, H])
        yacc = sb("yacc", [P, NT, H])
        xnT = sb("xnT", [P, KC, NB * L])
        xh = sb("xh", [P, KC, NB * L], F32R)
        xl = sb("xl", [P, KC, NB * L], F32R)
        delta = sb("delta", [P, KC, NB * L])
        u = sb("u", [P, KC, NB * L])
        soft = sb("soft", [P, KC, NB * L])
        proj = sb("proj", [PR, NB, L])
        wproj_s = sb("wproj_s", [P, KC, PR])
        wdt_s = sb("wdt_s", [R + 1, KC, P])
        A = sb("A", [P, KC * N])
        dsk = sb("dsk", [P, H])
        warm = sb("warm", [P, L], BF16)
        con = sb("con", [P, P + E * E + 1])
        ident = con[:, 0:P]
        lower = con[:, P:P + E * E].rearrange("p (a b) -> p a b", a=E)
        ones_row = con[0:PR, P + E * E:]
        sel = sb("sel", [SK, N * P + F], BF16)
        stats = sb("stats", [P, NT, 6])
        mv = sb("mv", [P, NT, 2])
        ve = sb("ve", [P, NT])
        sd = sb("sd", [P, NT])
        rs = sb("rs", [P, NT])
        rt = sb("rt", [P, NT])
        nm = sb("nm", [P, NT])
        sm = sb("sm", [P, NT, SM_B])
        rmx = sb("rmx", [P, NT])
        lg = sb("lg", [P, NT, E + 1])
        eg = sb("eg", [P, NT, E + 1])
        rsum = sb("rsum", [P, NT, 2])
        pr = sb("pr", [P, NT, E])
        beats = sb("beats", [P, TB, E, E])
        ties = sb("ties", [P, TB, E, E])
        rank = sb("rank", [P, TB, E])
        zt = sb("zt", [P, NT, PARTS, STP])
        zh = sb("zh", [P, TB, ROWS], BF16)
        stack = sb("stack", [SK, 1 + NB, L], BF16)
        bb = sb("bb", [P, 2, L])
        bx = sb("bx", [P, 2, KC, L])
        h = sb("h", [P, 2, KC, L])
        th = sb("th", [P, 2, L])
        us = sb("us", [P, 2, L])
        cb = sb("cb", [P, 2, L])
        ag = sb("ag", [P, 2, L])
        hid = sb("hid", [P, 2, L])
        wg_r = sb("wg_r", [P, 2, 2, KC, P])
        wg_h = sb("wg_h", [P, 2, 2, KC, P], F32R)
        wg_l = sb("wg_l", [P, 2, 2, KC, P], F32R)
        wd_r = sb("wd_r", [P, 2, H])

        x_in = sems("x_in", NB + 1)
        con_in, wproj_in, wdt_in = map(sem, ("con_in", "wproj_in", "wdt_in"))
        alog_in, dsk_in, sel_in = map(sem, ("alog_in", "dsk_in", "sel_in"))
        wg_in = sems("wg_in", 2)
        wd_in = sems("wd_in", 2)
        stored = sem("stored")
        dve_chain = sem("dve_chain")
        act_chain = sem("act_chain")
        ve_ready = sem("ve_ready")
        sd_ready = sem("sd_ready")
        nm_ready = sem("nm_ready")
        xn_dve = sem("xn_dve")
        xn_act = sem("xn_act")
        xnT_ps = sem("xnT_ps")
        xnT_ready = sems("xnT_ready", KC)
        xh_ready = sem("xh_ready")
        xl_ready = sem("xl_ready")
        sm_ps = sem("sm_ps")
        proj_ps = sem("proj_ps")
        proj_ready = sem("proj_ready")
        z_ps = sem("z_ps")
        z_abs = sem("z_abs")
        z_pos = sem("z_pos")
        soft_ready = sem("soft_ready")
        delta_ready = sem("delta_ready")
        u_ready_b = sems("u_ready_b", NB)
        pool_chain = sem("pool_chain")
        yinit_ready = sem("yinit_ready")
        warm_ready = sem("warm_ready")
        zt_zero = sem("zt_zero")
        A_exp = sem("A_exp")
        A_ready = sem("A_ready")
        lg_ready = sem("lg_ready")
        eg_ready = sem("eg_ready")
        zt_ready = sem("zt_ready")
        zt_ps = sem("zt_ps")
        sm_copied = sem("sm_copied")
        stack_ready = sem("stack_ready")
        b_ps = sem("b_ps")
        b_copied = sem("b_copied")
        bx_ready = sem("bx_ready")
        c_ps = sem("c_ps")
        c_copied = sem("c_copied")
        dA_ready = sem("dA_ready")
        scanned = sem("scanned")
        hT_ready = sem("hT_ready")
        y_added = sem("y_added")
        wh_ready = sem("wh_ready")
        wl_first = sems("wl_first", 2)
        wl_ready = sem("wl_ready")
        g_ready = sem("g_ready")
        u_ready = sem("u_ready")
        tanh_ready = sem("tanh_ready")
        us_ready = sem("us_ready")
        ag_ready = sem("ag_ready")
        q_ready = sem("q_ready")
        hid_ready = sem("hid_ready")
        hid_last = sem("hid_last")
        half_down = sem("half_down")
        down_done = sem("down_done")
        y_final = sem("y_final")

        TURNED, FULL = (0, HT), (0, HT)
        PROJ, SMALL = (GB, HT), (UB, HT + 1)
        TURNED_PARTS = (ACC + 1, ACC + 1, DA)
        STACK_B, STACK_C = (0, 2), (1, 2)
        hT = ps[:, HT:HT + 2, :].rearrange("p a (j d) -> p (a j) d", d=H)
        acc = ps[:, ACC:ACC + 2, :].rearrange("p a (j d) -> p (a j) d", d=H)

        def tiles(b):
            return slice(TB * b, TB * b + TB)

        def tokens(b):
            return slice(L * b, L * b + L)

        def state(b, n0, i):
            return N * b + n0 + 2 * i

        def chunk(b, n0, i):
            return (N + 1) * b + n0 + 2 * i

        def chunk_slot(b, n0):
            return ((N + 1) * b + n0) % 2

        def chunk_use(b, n0, i):
            return ((N + 1) * b + n0) // 2 + i + 1

        def after(b, n0):
            return (b, n0 + 1) if n0 < N else (b + 1, 0)

        def rows_of(n0):
            return P if n0 < N else TAIL

        def halves(b, n0):
            return (slice(0, L // 2), slice(L // 2, L)) if (b, n0) == (NB - 1, N) else (slice(0, L),)

        def steps(eng, b, step, between=lambda b, n0: None):
            for n0 in range(2):
                step(b, n0, 0)
                between(b, n0)
            with eng.Fori(0, N // 2 - 2) as i:
                step(b, 2, i)
                step(b, 3, i)
            for n0 in range(N - 2, N + 1):
                step(b, n0, 0)
                between(b, n0)

        block = ctx.enter_context(nc.Block())

        @block.sync
        def _(sp):
            xv = x.rearrange("(t p) d -> p t d", p=P)
            ov = out.rearrange("(t p) d -> p t d", p=P)
            for k in range(2):
                t = slice(2 * k, 2 * k + 2)
                sp.dma_start(xt[:, t, :], xv[:, t, :]).then_inc(x_in[k], 16)
            sp.dma_start(con[:, :], consts).then_inc(con_in, 16)
            sp.dma_start(wproj_s[:, :, :], wproj).then_inc(wproj_in, 16)
            sp.dma_start(wdt_s[:, :, :], wdt).then_inc(wdt_in, 16)

            def load_gate_up(b, n0, i):
                m, slot = chunk(b, n0, i), chunk_slot(b, n0)
                if b == 0 and n0 in (2, 3):
                    sp.wait_ge(wl_first[slot], 1)
                elif not (b == 0 and n0 < 2):
                    sp.wait_ge(wl_ready, m - 3)
                if n0 == N:
                    sp.dma_start(wg_r[:, slot, :, :, 0:TAIL], wgu_tail).then_inc(wg_in[slot], 16)
                else:
                    src = wgu[bass.ds(n0 + 2 * i, 1)].rearrange("a p g k f -> (a p) g k f")
                    sp.dma_start(wg_r[:, slot, :, :, :], src).then_inc(wg_in[slot], 16)

            def load_down(b, n0, i):
                m, slot = chunk(b, n0, i), chunk_slot(b, n0)
                if not (b == 0 and n0 < 2):
                    sp.wait_ge(down_done, m - 1)
                if n0 == N:
                    sp.dma_start(wd_r[0:TAIL, slot, :], wd[N * P:F, :]).then_inc(wd_in[slot], 16)
                else:
                    sp.dma_start(wd_r[:, slot, :], wd[bass.ds((n0 + 2 * i) * P, P), :]).then_inc(wd_in[slot], 16)

            def store(b):
                for k in range(2):
                    t = slice(TB * b + 2 * k, TB * b + 2 * k + 2)
                    sp.wait_ge(y_final, 2 * b + k + 1)
                    sp.dma_start(ov[:, t, :], yacc[:, t, :]).then_inc(stored, 16)

            load_gate_up(0, 0, 0)
            sp.dma_start(xt[:, tiles(1), :], xv[:, tiles(1), :]).then_inc(x_in[2], 16)
            for b in range(NB):
                for n0 in range(4):
                    if (b, n0) != (0, 0):
                        load_gate_up(b, n0, 0)
                    if n0 > 0:
                        load_down(b, n0 - 1, 0)
                    elif b:
                        load_down(b - 1, N, 0)
                if b:
                    store(b - 1)
                with sp.Fori(0, N // 2 - 2) as i:
                    for n0 in (4, 5):
                        load_gate_up(b, n0, i)
                        load_down(b, n0 - 1, i)
                load_gate_up(b, N, 0)
                load_down(b, N - 1, 0)
            load_down(NB - 1, N, 0)
            store(NB - 1)
            sp.wait_ge(stored, 16 * 2 * NB)

        @block.gpsimd
        def _(pool):
            def low_x(b):
                c = tokens(b)
                pool.wait_ge(xh_ready, b + 1)
                pool.tensor_tensor(xl[:, :, c], xnT[:, :, c], xh[:, :, c].bitcast(F32), ALU.subtract)\
                    .then_inc(xl_ready, 1)

            def low_w(n0):
                pool.wait_ge(wh_ready, n0 + 1)
                pool.tensor_tensor(wg_l[:, n0, :, :, :], wg_r[:, n0, :, :, :],
                                   wg_h[:, n0, :, :, :].bitcast(F32), ALU.subtract).then_inc(wl_first[n0], 1)

            def start_y(b):
                t = tiles(b)
                pool.wait_ge(xn_dve, 2 * (b + 1))
                pool.wait_ge(xn_act, 2 * (b + 1))
                pool.tensor_tensor(yacc[:, t, :], xn[:, t, :], dsk[:, None, :].to_broadcast([P, TB, H]),
                                   ALU.mult).then_inc(pool_chain, 1)
                if b == 0:
                    pool.wait_ge(pool_chain, 1)
                    pool.tensor_tensor(yacc[:, t, :], yacc[:, t, :], xt[:, t, :], ALU.add).then_inc(yinit_ready, 1)

            def drift(b):
                c = tokens(b)
                pool.wait_ge(delta_ready, KC * (b + 1))
                pool.tensor_tensor(u[:, :, c], delta[:, :, c], xnT[:, :, c], ALU.mult).then_inc(u_ready_b[b], 1)

            def drive(b, n0, i):
                s = state(b, n0, i)
                slot = n0 % 2
                pool.wait_ge(b_copied, s + 1)
                if not (b == 0 and n0 < 2):
                    pool.wait_ge(scanned, KC * (s - 1))
                if n0 == 0:
                    pool.wait_ge(u_ready_b[b], 1)
                bs = bb[:, slot, :]
                pool.tensor_tensor(bx[:, slot, :, :], u[:, :, tokens(b)],
                                   bs[:, None, :].to_broadcast([P, KC, L]), ALU.mult).then_inc(bx_ready, 1)

            def weigh(b, n0, i):
                m, slot, r = chunk(b, n0, i), chunk_slot(b, n0), rows_of(n0)
                pool.wait_ge(us_ready, m + 1)
                pool.wait_ge(c_copied, m + 1)
                pool.tensor_tensor(us[0:r, slot, :], us[0:r, slot, :], cb[0:r, slot, :], ALU.mult)\
                    .then_inc(q_ready, 1)

            def hidden(b, n0, i):
                m, slot, r = chunk(b, n0, i), chunk_slot(b, n0), rows_of(n0)
                pool.wait_ge(q_ready, m + 1)
                pool.wait_ge(ag_ready, m + 1)
                if not (b == 0 and n0 < 2):
                    pool.wait_ge(down_done, m - 1)
                if b == NB - 1 and n0 == N:
                    return
                pool.tensor_tensor(hid[0:r, slot, :], ag[0:r, slot, :], us[0:r, slot, :], ALU.mult)\
                    .then_inc(hid_ready, 1)

            def step(b, n0, i):
                nb, nn = after(b, n0)
                if not (b == 0 and n0 == 0):
                    weigh(b, n0, i)
                if nn < N and nb < NB:
                    drive(nb, nn, i)
                if b == 0 and n0 == 0:
                    weigh(b, n0, i)
                hidden(b, n0, i)

            def between(b, n0):
                if b + 1 < NB and n0 == N - 2:
                    low_x(b + 1)
                if b + 1 < NB and n0 == N - 1:
                    drift(b + 1)

            pool.memset(warm[:, :], 0.0).then_inc(warm_ready, 1)
            pool.memset(zt[:, :, :, :], 0.0).then_inc(zt_zero, 1)
            low_w(0)
            low_x(0)
            low_w(1)
            pool.wait_ge(dsk_in, 16)
            start_y(0)
            start_y(1)
            drive(0, 0, 0)
            for b in range(NB):
                steps(pool, b, step, between)

        @block.scalar
        def _(act):
            act.dma_start(A[:, :], alog).then_inc(alog_in, 16)
            act.dma_start(dsk[:, :], dskip[None, :].to_broadcast([P, H])).then_inc(dsk_in, 16)
            def root(b):
                act.wait_ge(ve_ready, b + 1)
                act.activation(sd[:, tiles(b)], ve[:, tiles(b)], ACT.Sqrt).then_inc(sd_ready, 1)

            def normalise(b):
                act.wait_ge(nm_ready, b + 1)
                for t in range(TB * b + 2, TB * b + 4):
                    act.activation(xn[:, t, :], xt[:, t, :], ACT.Identity, bias=nm[:, t:t + 1], scale=rs[:, t:t + 1])\
                       .then_inc(xn_act, 1)

            def turned_x(b):
                act.wait_ge(xnT_ps, b + 1)
                act.activation(xnT[:, 1, tokens(b)], ps[:, TURNED[b] + 1, :], ACT.Copy).then_inc(xnT_ready[1], 1)

            def high_x(b):
                for kc in range(KC):
                    act.wait_ge(xnT_ready[kc], b + 1)
                act.activation(xh[:, :, tokens(b)], xnT[:, :, tokens(b)], ACT.Copy).then_inc(xh_ready, 1)

            def make_stack(k):
                act.wait_ge(zt_ps, k + 1)
                act.activation(stack[:, k, :], ps[0:SK, TURNED_PARTS[k], :], ACT.Copy).then_inc(stack_ready, 1)

            def high_w(b, n0, i):
                m, slot = chunk(b, n0, i), chunk_slot(b, n0)
                w = slice(0, rows_of(n0))
                act.wait_ge(wg_in[slot], 16 * chunk_use(b, n0, i))
                if not (b == 0 and n0 < 2):
                    act.wait_ge(g_ready, m - 1)
                act.activation(wg_h[:, slot, :, :, w], wg_r[:, slot, :, :, w], ACT.Copy).then_inc(wh_ready, 1)

            def soft_abs(b):
                for kc in range(KC):
                    act.wait_ge(z_ps, KC * b + kc + 1)
                    act.activation(soft[:, kc, tokens(b)], ps[:, FULL[b] + kc, :], ACT.Abs).then_inc(z_abs, 1)

            def soft_exp(b):
                c = soft[:, :, tokens(b)]
                act.wait_ge(z_abs, KC * (b + 1))
                act.activation(c, c, ACT.Exp, scale=-1.0).then_inc(act_chain, 1)

            def soft_log(b):
                act.wait_ge(act_chain, b + 1)
                for kc in range(KC):
                    c = soft[:, kc, tokens(b)]
                    act.activation(c, c, ACT.Ln, bias=1.0).then_inc(soft_ready, 1)

            def router_exp(b):
                act.wait_ge(lg_ready, b + 1)
                act.activation(eg[:, tiles(b), :], lg[:, tiles(b), :], ACT.Exp).then_inc(eg_ready, 1)

            def b_copy(b, n0, i):
                s = state(b, n0, i)
                act.wait_ge(b_ps, s + 1)
                if not (b == 0 and n0 < 2):
                    act.wait_ge(bx_ready, s - 1)
                act.activation(bb[:, n0 % 2, :], ps[:, UB, :], ACT.Copy).then_inc(b_copied, 1)

            def decay(b, n0, i, kc):
                s = state(b, n0, i)
                if n0 == 0:
                    act.wait_ge(delta_ready, KC * b + kc + 1)
                if n0 == 0 and b:
                    act.wait_ge(stack_ready, 3)
                if b == 0 and n0 == 0:
                    act.wait_ge(A_ready, 1)
                else:
                    act.wait_ge(scanned, KC * (s - 1) + kc + 1)
                n = n0 + 2 * i
                act.activation(ps[:, DA + kc, :], delta[:, kc, tokens(b)], ACT.Exp,
                               scale=A[:, bass.ds(kc * N + n, 1)]).then_inc(dA_ready, 1)

            def c_copy(b, n0, i):
                m, slot, r = chunk(b, n0, i), chunk_slot(b, n0), rows_of(n0)
                act.wait_ge(c_ps, m + 1)
                if not (b == 0 and n0 < 2):
                    act.wait_ge(q_ready, m - 1)
                act.activation(cb[0:r, slot, :], ps[0:r, UB, :], ACT.Copy).then_inc(c_copied, 1)

            def halve_up(b, n0, i):
                m, slot, r = chunk(b, n0, i), chunk_slot(b, n0), rows_of(n0)
                act.wait_ge(u_ready, m + 1)
                if not (b == 0 and n0 < 2):
                    act.wait_ge(hid_ready, m - 1)
                act.activation(us[0:r, slot, :], ps[0:r, UB, :], ACT.Copy, scale=0.5).then_inc(us_ready, 1)

            def tanh(b, n0, i):
                m, slot, r = chunk(b, n0, i), chunk_slot(b, n0), rows_of(n0)
                act.wait_ge(g_ready, m + 1)
                if not (b == 0 and n0 < 2):
                    act.wait_ge(ag_ready, m - 1)
                act.activation(th[0:r, slot, :], ps[0:r, GB, :], ACT.Tanh, scale=0.5).then_inc(tanh_ready, 1)

            def step(b, n0, i):
                nb, nn = after(b, n0)
                scans = nn < N and nb < NB
                if b == 0 and n0 == 0:
                    c_copy(nb, nn, i)
                    soft_abs(NB - 1)
                    for kc in range(KC):
                        decay(nb, nn, i, kc)
                    return
                if b == 0 and n0 == 1:
                    halve_up(b, n0, i)
                if nb < NB:
                    high_w(nb, nn, i)
                if b + 1 < NB and n0 == N - 1:
                    soft_log(b + 1)
                if not (b == 0 and n0 == 1):
                    halve_up(b, n0, i)
                if b + 1 < NB and n0 == N:
                    make_stack(2)
                if scans:
                    decay(nb, nn, i, 0)
                tanh(b, n0, i)
                if scans:
                    b_copy(nb, nn, i)
                    decay(nb, nn, i, 1)
                if nb < NB:
                    c_copy(nb, nn, i)

            def between(b, n0):
                if b + 1 < NB and n0 == 1:
                    router_exp(b + 1)
                    high_x(b + 1)
                    soft_exp(b + 1)

            root(0)
            act.dma_start(sel[:, :], selectors).then_inc(sel_in, 16)
            normalise(0)
            high_w(0, 0, 0)
            turned_x(0)
            high_x(0)
            high_w(0, 1, 0)
            root(1)
            act.wait_ge(alog_in, 16)
            act.activation(A[:, :], A[:, :], ACT.Exp).then_inc(A_exp, 1)
            normalise(1)
            router_exp(0)
            soft_abs(0)
            soft_exp(0)
            soft_log(0)
            turned_x(1)
            make_stack(0)
            halve_up(0, 0, 0)
            tanh(0, 0, 0)
            b_copy(0, 0, 0)
            decay(0, 0, 0, 0)
            b_copy(0, 1, 0)
            make_stack(1)
            c_copy(0, 0, 0)
            decay(0, 0, 0, 1)
            for b in range(NB):
                steps(act, b, step, between)

        @block.vector
        def _(dve):
            chain = [0]

            def link(ins):
                chain[0] += 1
                ins.then_inc(dve_chain, 1)
                dve.wait_ge(dve_chain, chain[0])

            def moments(b):
                t = tiles(b)
                for k in range(TB * b, TB * b + TB):
                    if k == 0 or k == 2 or k == TB:
                        dve.wait_ge(x_in[k // 2], 16)
                    last = dve.bn_stats(stats[:, k, :], xt[:, k, :])
                link(last)
                for k in range(TB * b, TB * b + TB):
                    last = dve.bn_aggr(mv[:, k, :], stats[:, k, :])
                link(last)
                dve.tensor_scalar(ve[:, t], mv[:, t, 1], EPS, None, ALU.add).then_inc(ve_ready, 1)

            def roots(b):
                t = tiles(b)
                dve.wait_ge(sd_ready, b + 1)
                link(dve.reciprocal(rs[:, t], sd[:, t]))
                link(dve.tensor_tensor(rt[:, t], rs[:, t], rs[:, t], ALU.mult))
                link(dve.tensor_tensor(rt[:, t], rt[:, t], ve[:, t], ALU.mult))
                link(dve.tensor_scalar(rt[:, t], rt[:, t], -0.5, 1.5, ALU.mult, ALU.add))
                link(dve.tensor_tensor(rs[:, t], rs[:, t], rt[:, t], ALU.mult))
                dve.scalar_tensor_tensor(nm[:, t], mv[:, t, 0], -1.0, rs[:, t], ALU.mult, ALU.mult)\
                   .then_inc(nm_ready, 1)

            def normalise(b):
                for k in range(TB * b, TB * b + 2):
                    dve.tensor_scalar(xn[:, k, :], xt[:, k, :], mv[:, k, 0:1], rs[:, k:k + 1],
                                      ALU.subtract, ALU.mult).then_inc(xn_dve, 1)

            def turned_x(b):
                dve.wait_ge(xnT_ps, b + 1)
                dve.tensor_copy(xnT[:, 0, tokens(b)], ps[:, TURNED[b], :]).then_inc(xnT_ready[0], 1)

            def parts(b, rows):
                t, w = tiles(b), rows.stop - rows.start
                link(dve.tensor_copy(zh[:, :, 0:w], zt[:, t, 0, rows]))
                link(dve.tensor_tensor(zt[:, t, 1, rows], zt[:, t, 0, rows], zh[:, :, 0:w], ALU.subtract))
                link(dve.tensor_copy(zh[:, :, 0:w], zt[:, t, 1, rows]))
                dve.tensor_tensor(zt[:, t, 2, rows], zt[:, t, 1, rows], zh[:, :, 0:w], ALU.subtract)\
                   .then_inc(zt_ready, 1)

            def positive(b):
                for kc in range(KC):
                    dve.wait_ge(z_abs, KC * b + kc + 1)
                    dve.tensor_scalar(delta[:, kc, tokens(b)], ps[:, FULL[b] + kc, :], 0.0, None, ALU.max)\
                       .then_inc(z_pos, 1)

            def make_delta(b):
                for kc in range(KC):
                    c = delta[:, kc, tokens(b)]
                    dve.wait_ge(soft_ready, KC * b + kc + 1)
                    if b == 0:
                        dve.wait_ge(z_abs, kc + 1)
                        dve.scalar_tensor_tensor(c, ps[:, FULL[b] + kc, :], 0.0, soft[:, kc, tokens(b)],
                                                 ALU.max, ALU.add).then_inc(delta_ready, 1)
                    else:
                        dve.wait_ge(z_pos, kc + 1)
                        dve.tensor_tensor(c, c, soft[:, kc, tokens(b)], ALU.add).then_inc(delta_ready, 1)

            def copy_proj(b):
                dve.wait_ge(proj_ps, b + 1)
                dve.tensor_scalar(proj[:, b, :], ps[0:PR, PROJ[b], :], ones_row, None, ALU.add)\
                   .then_inc(proj_ready, 1)

            def copy_small(b):
                t = tiles(b)
                dve.wait_ge(sm_ps, b + 1)
                small = ps[:, SMALL[b], :].rearrange("p (t c) -> p t c", t=TB)[:, :, R + 1:PR]
                dve.tensor_copy(zt[:, t, 0, ROW_B:ROWS], small[:, :, SM_B:SM])
                dve.tensor_copy(sm[:, t, :], small[:, :, 0:SM_B]).then_inc(sm_copied, 1)

            def logits(b):
                t = tiles(b)
                dve.wait_ge(sm_copied, b + 1)
                link(dve.tensor_reduce(rmx[:, t], sm[:, t, SM_R:SM_R + E], AX.X, ALU.max))
                dve.tensor_tensor(lg[:, t, 0:E], sm[:, t, SM_R:SM_R + E], rmx[:, t, None].to_broadcast([P, TB, E]),
                                  ALU.subtract)
                dve.tensor_scalar(lg[:, t, E], sm[:, t, SM_G], -1.0, 80.0, ALU.mult, ALU.min).then_inc(lg_ready, 1)

            def route(b):
                t = tiles(b)
                dve.wait_ge(eg_ready, b + 1)
                dve.tensor_reduce(rsum[:, t, 0], eg[:, t, 0:E], AX.X, ALU.add)
                link(dve.tensor_scalar(rsum[:, t, 1], eg[:, t, E], 1.0, None, ALU.add))
                link(dve.reciprocal(rsum[:, t, :], rsum[:, t, :]))
                if b == 0:
                    dve.wait_ge(zt_ps, 1)
                dve.tensor_copy(zt[:, t, 0, 0], rsum[:, t, 1])
                link(dve.tensor_tensor(pr[:, t, :], eg[:, t, 0:E], rsum[:, t, 0:1].to_broadcast([P, TB, E]),
                                       ALU.mult))
                other = pr[:, t, None, :].to_broadcast([P, TB, E, E])
                own = pr[:, t, :, None].to_broadcast([P, TB, E, E])
                dve.tensor_tensor(beats[:, :, :, :], other, own, ALU.is_gt)
                link(dve.tensor_tensor(ties[:, :, :, :], other, own, ALU.is_equal))

            def select(b):
                t = tiles(b)
                link(dve.tensor_tensor(ties[:, :, :, :], ties[:, :, :, :],
                                       lower[:, None, :, :].to_broadcast([P, TB, E, E]), ALU.mult))
                link(dve.tensor_tensor(beats[:, :, :, :], beats[:, :, :, :], ties[:, :, :, :], ALU.add))
                link(dve.tensor_reduce(rank[:, :, :], beats[:, :, :, :], AX.X, ALU.add))
                link(dve.scalar_tensor_tensor(zt[:, t, 0, 1:1 + E], rank[:, :, :], float(TOPK), pr[:, t, :],
                                              ALU.is_lt, ALU.mult))

            def low_w(b, n0, i):
                m, slot = chunk(b, n0, i), chunk_slot(b, n0)
                w = slice(0, rows_of(n0))
                dve.wait_ge(wh_ready, m + 1)
                dve.tensor_tensor(wg_l[:, slot, :, :, w], wg_r[:, slot, :, :, w],
                                  wg_h[:, slot, :, :, w].bitcast(F32), ALU.subtract).then_inc(wl_ready, 1)

            def scan(b, n0, i):
                s, slot = state(b, n0, i), n0 % 2
                dve.wait_ge(bx_ready, s + 1)
                if not (b == 0 and n0 < 2):
                    dve.wait_ge(hT_ready, s - 1)
                for kc in range(KC):
                    dve.wait_ge(dA_ready, KC * s + kc + 1)
                    dve.tensor_tensor_scan(h[:, slot, kc, :], ps[:, DA + kc, :], bx[:, slot, kc, :], 0.0,
                                           ALU.mult, ALU.add).then_inc(scanned, 1)

            def add_y(b, n0, i):
                s = state(b, n0, i)
                n = n0 + 2 * i
                dve.wait_ge(hT_ready, s + 1)
                if n0 > 0:
                    dve.wait_ge(y_added, s)
                elif b == 0:
                    dve.wait_ge(yinit_ready, 1)
                for j in range(TB):
                    t = TB * b + j
                    last = dve.scalar_tensor_tensor(yacc[:, t, :], hT[:, j, :], sm[:, t, bass.ds(SM_C + n, 1)],
                                                    yacc[:, t, :], ALU.mult, ALU.add)
                last.then_inc(y_added, 1)

            def silu(b, n0, i):
                m, slot, r = chunk(b, n0, i), chunk_slot(b, n0), rows_of(n0)
                dve.wait_ge(tanh_ready, m + 1)
                last = b == NB - 1 and n0 == N
                if not (b == 0 and n0 < 2):
                    dve.wait_ge(hid_ready, m - 1)
                for k, c in enumerate(halves(b, n0)):
                    dve.scalar_tensor_tensor(ag[0:r, slot, c], th[0:r, slot, c], 1.0, ps[0:r, GB, c],
                                             ALU.add, ALU.mult).then_inc(ag_ready, 1)
                    if last:
                        dve.wait_ge(ag_ready, m + 1 + k)
                        dve.wait_ge(q_ready, m + 1)
                        dve.wait_ge(down_done, m - 1)
                        dve.tensor_tensor(hid[0:r, slot, c], ag[0:r, slot, c], us[0:r, slot, c], ALU.mult)\
                           .then_inc(hid_last, 1)

            def start_y(b):
                t = tiles(b)
                dve.wait_ge(pool_chain, b + 1)
                link(dve.tensor_tensor(yacc[:, t, :], yacc[:, t, :], xt[:, t, :], ALU.add))

            def finish(b):
                dve.wait_ge(y_added, N * (b + 1))
                for k in range(2):
                    if b == NB - 1 and k == 0:
                        dve.wait_ge(half_down, 1)
                    else:
                        dve.wait_ge(down_done, (N + 1) * (b + 1))
                    t = slice(TB * b + 2 * k, TB * b + 2 * k + 2)
                    dve.tensor_tensor(yacc[:, t, :], yacc[:, t, :], acc[:, 2 * k:2 * k + 2, :], ALU.add)\
                       .then_inc(y_final, 1)

            def step(b, n0, i):
                nb, nn = after(b, n0)
                if n0 < N:
                    scan(b, n0, i)
                if n0 > 0:
                    add_y(b, n0 - 1, i)
                if nb < NB and not (b == 0 and n0 == 0):
                    low_w(nb, nn, i)
                if b + 1 < NB and n0 == N - 1:
                    make_delta(b + 1)
                if not (b == 0 and n0 == 0):
                    silu(b, n0, i)

            def between(b, n0):
                if b and n0 == 0:
                    finish(b - 1)
                if b + 1 < NB and n0 == 0:
                    positive(b + 1)
                    logits(b + 1)
                if b + 1 < NB and n0 == 1:
                    route(b + 1)
                if b + 1 < NB and n0 == N - 2:
                    select(b + 1)
                if b + 1 < NB and n0 == N - 1:
                    parts(b + 1, slice(0, ROWS))
                if b + 1 < NB and n0 == N:
                    start_y(b + 1)

            moments(0)
            roots(0)
            normalise(0)
            turned_x(0)
            moments(1)
            dve.wait_ge(con_in, 16)
            copy_proj(0)
            roots(1)
            dve.wait_ge(zt_zero, 1)
            copy_small(0)
            logits(0)
            parts(0, slice(ROW_B, ROWS))
            normalise(1)
            dve.wait_ge(A_exp, 1)
            dve.tensor_scalar(A[:, :], A[:, :], -1.0, None, ALU.mult).then_inc(A_ready, 1)
            route(0)
            turned_x(1)
            select(0)
            make_delta(0)
            copy_proj(1)
            dve.wait_ge(delta_ready, KC)
            dve.tensor_tensor(u[:, :, tokens(0)], delta[:, :, tokens(0)], xnT[:, :, tokens(0)], ALU.mult)\
               .then_inc(u_ready_b[0], 1)
            parts(0, slice(0, ROW_B))
            copy_small(1)
            silu(0, 0, 0)
            for b in range(NB):
                steps(dve, b, step, between)
            finish(NB - 1)

        @block.tensor
        def _(pe):
            def turn_x(b):
                for j in range(TB):
                    if j < 2:
                        pe.wait_ge(xn_dve, 2 * b + j + 1)
                    else:
                        pe.wait_ge(xn_act, 2 * b + j - 1)
                    for kc in range(KC):
                        last = pe.transpose(ps[:, TURNED[b] + kc, j * P:(j + 1) * P],
                                            xn[:, TB * b + j, kc * P:(kc + 1) * P], ident)
                last.then_inc(xnT_ps, 1)

            def project_x(b):
                for kc in range(KC):
                    pe.wait_ge(xnT_ready[kc], b + 1)
                    last = pe.matmul(ps[0:PR, PROJ[b], :], wproj_s[:, kc, :], xnT[:, kc, tokens(b)],
                                     start=kc == 0, stop=kc == KC - 1)
                last.then_inc(proj_ps, 1)

            def full_rank(b, kcs=range(KC)):
                pe.wait_ge(proj_ready, b + 1)
                for kc in kcs:
                    pe.matmul(ps[:, FULL[b] + kc, :], wdt_s[:, kc, :], proj[0:R + 1, b, :], start=True, stop=True)\
                      .then_inc(z_ps, 1)

            def turn_small(b):
                pe.wait_ge(proj_ready, b + 1)
                for j in range(TB):
                    last = pe.transpose(ps[:, SMALL[b], P * j:P * j + PR], proj[:, b, j * P:(j + 1) * P],
                                        ident[0:PR, 0:PR])
                last.then_inc(sm_ps, 1)

            def turn_parts(k):
                b = (0, 0, 1)[k]
                pe.wait_ge(zt_ready, k + 1)
                for j in range(TB):
                    last = pe.transpose(ps[0:SK, TURNED_PARTS[k], j * P:(j + 1) * P],
                                        zt[:, TB * b + j, :, :].rearrange("p a c -> p (a c)"), ident)
                last.then_inc(zt_ps, 1)

            def spread_b(b, n0, i):
                n = n0 + 2 * i
                if n0 == 0:
                    pe.wait_ge(stack_ready, STACK_B[b] + 1)
                pe.matmul(ps[:, UB, :], sel[:, bass.ds(n * P, P)], stack[:, STACK_B[b], :],
                          start=True, stop=True).then_inc(b_ps, 1)

            def spread_c(b, n0, i):
                n, r = n0 + 2 * i, rows_of(n0)
                if n0 == 0:
                    pe.wait_ge(stack_ready, STACK_C[b] + 1)
                pe.matmul(ps[0:r, UB, :], sel[:, bass.ds(N * P + n * P, r)], stack[:, STACK_C[b], :],
                          start=True, stop=True).then_inc(c_ps, 1)

            def turn_h(b, n0, i):
                s, slot = state(b, n0, i), n0 % 2
                pe.wait_ge(scanned, KC * (s + 1))
                if b == 0 and n0 == 0:
                    pe.wait_ge(z_pos, KC)
                else:
                    pe.wait_ge(y_added, s)
                for j in range(TB):
                    for kc in range(KC):
                        last = pe.transpose(hT[:, j, kc * P:(kc + 1) * P], h[:, slot, kc, j * P:(j + 1) * P], ident)
                last.then_inc(hT_ready, 1)

            def project(b, n0, which, kcs=range(KC)):
                slot = chunk_slot(b, n0)
                bank, done = ((GB, g_ready), (UB, u_ready))[which]
                c = tokens(b)
                for kc in kcs:
                    for k, (w, xs) in enumerate(((wg_h, xh), (wg_h, xl), (wg_l, xh))):
                        last = pe.matmul(ps[:, bank, :], w[:, slot, which, kc, :], xs[:, kc, c],
                                         start=kc == 0 and k == 0, stop=kc == KC - 1 and k == 2)
                if KC - 1 in kcs:
                    last.then_inc(done, 1)

            def down(b, n0, i, js=range(TB)):
                m, slot, r = chunk(b, n0, i), chunk_slot(b, n0), rows_of(n0)
                first = n0 == 0
                if first and b:
                    pe.wait_ge(y_final, 2 * b)
                if first and not b:
                    pe.wait_ge(stack_ready, 2)
                if not (b == NB - 1 and n0 == N):
                    pe.wait_ge(hid_ready, m + 1)
                pe.wait_ge(wd_in[slot], 16 * chunk_use(b, n0, i))
                for j in js:
                    if b == NB - 1 and n0 == N and j % 2 == 0:
                        pe.wait_ge(hid_last, j // 2 + 1)
                    last = pe.matmul(acc[:, j, :], hid[0:r, slot, j * P:(j + 1) * P], wd_r[0:r, slot, :],
                                     start=first and j % 2 == 0, stop=True, skip_group_check=True)
                    if b == NB - 1 and n0 == N and j == 1:
                        last.then_inc(half_down, 1)
                if TB - 1 in js:
                    last.then_inc(down_done, 1)

            def up_gate(b, n0, i):
                m, slot = chunk(b, n0, i), chunk_slot(b, n0)
                if n0 == 0:
                    pe.wait_ge(xl_ready, b + 1)
                if b == 0 and n0 == 0:
                    pe.wait_ge(wl_first[0], 1)
                elif not (b == 0 and n0 == 1):
                    pe.wait_ge(wl_ready, m - 1)
                project(b, n0, 1)
                if b + 1 < NB and n0 == N:
                    turn_parts(2)
                if b == 0 and n0 == 1:
                    return
                if not (b == 0 and n0 == 0):
                    pe.wait_ge(ag_ready, m)
                project(b, n0, 0)

            def step(b, n0, i):
                m = chunk(b, n0, i)
                nb, nn = after(b, n0)
                scans = nn < N and nb < NB
                if not (b == 0 and n0 == 0):
                    pe.wait_ge(c_copied, m + 1)
                    up_gate(b, n0, i)
                    if b == 0 and n0 == 1:
                        turn_h(0, 0, 0)
                    pe.wait_ge(us_ready, m + 1)
                    if scans:
                        spread_b(nb, nn, i)
                    if b + 1 < NB and n0 == N:
                        down(b, n0 - 1, i, range(2))
                        pe.wait_ge(b_copied, state(nb, nn, i) + 1)
                        spread_c(nb, nn, i)
                        down(b, n0 - 1, i, range(2, TB))
                        return
                    if n0 > 0:
                        down(b, n0 - 1, i)
                    else:
                        down(b - 1, N, 0)
                    if nb < NB:
                        if scans:
                            pe.wait_ge(b_copied, state(nb, nn, i) + 1)
                        spread_c(nb, nn, i)
                if n0 < N and not (b == 0 and n0 == 0):
                    turn_h(b, n0, i)

            def wake(count):
                for k in range(count):
                    pe.matmul(ps[:, ACC, :], warm[:, 0:P], warm[:, :], start=True, stop=True)

            pe.wait_ge(warm_ready, 1)
            wake(WARM)
            pe.wait_ge(con_in, 16)
            turn_x(0)
            wake(3)
            pe.wait_ge(wproj_in, 16)
            project_x(0)
            wake(4)
            turn_small(0)
            pe.wait_ge(wdt_in, 16)
            full_rank(0)
            turn_parts(0)
            turn_x(1)
            pe.wait_ge(sm_copied, 1)
            up_gate(0, 0, 0)
            project_x(1)
            pe.wait_ge(sel_in, 16)
            pe.wait_ge(us_ready, 1)
            spread_b(0, 0, 0)
            wake(3)
            turn_small(1)
            full_rank(1, range(1))
            pe.wait_ge(b_copied, 1)
            spread_b(0, 1, 0)
            pe.wait_ge(stack_ready, 1)
            turn_parts(1)
            pe.wait_ge(sm_copied, 2)
            full_rank(1, range(1, KC))
            pe.wait_ge(b_copied, 2)
            spread_c(0, 0, 0)
            pe.wait_ge(ag_ready, 1)
            pe.wait_ge(wl_first[1], 1)
            project(0, 1, 0, range(1))
            pe.wait_ge(c_copied, 1)
            spread_c(0, 1, 0)
            project(0, 1, 0, range(1, KC))
            for b in range(NB):
                steps(pe, b, step)
            down(NB - 1, N, 0)


def kernel(L0_attn_x, L0_attn_W_xproj, L0_attn_W_dt, L0_attn_b_dt, L0_attn_A_log, L0_attn_D, L0_ffn_Wr,
           L0_ffn_Wg, L0_ffn_Wu, L0_ffn_Wd, L0_ffn_Sg, L0_ffn_Su, L0_ffn_Sd, L0_ffn_Wsg):
    import ml_dtypes
    import numpy as np
    import concourse.bacc as bacc
    from concourse.bass_utils import run_bass_kernel_spmd

    def f(a):
        return np.asarray(a)

    wx = f(L0_attn_W_xproj)
    gate = np.concatenate([f(L0_ffn_Sg), f(L0_ffn_Wg).transpose(1, 0, 2).reshape(H, E * FE)], axis=1)
    up = np.concatenate([f(L0_ffn_Su), f(L0_ffn_Wu).transpose(1, 0, 2).reshape(H, E * FE)], axis=1)
    gu = np.stack([gate, up]).reshape(2, KC, P, F).transpose(2, 0, 1, 3)
    consts = np.concatenate([np.eye(P, dtype=np.float32),
                             np.tile(np.tril(np.ones((E, E), np.float32), -1).reshape(1, E * E), (P, 1)),
                             np.arange(P)[:, None] == R], axis=1).astype(np.float32)
    unit = np.arange(F)
    owner = np.where(unit < FS, 0, 1 + (unit - FS) // FE)
    picked = np.concatenate([np.repeat(ROW_B + np.arange(N), P), owner])
    selectors = (np.arange(SK)[:, None] % STP == picked[None, :]).astype(ml_dtypes.bfloat16)

    arrays = {
        "x": f(L0_attn_x).reshape(NB * L, H),
        "wgu": gu[..., :N * P].reshape(P, 2, KC, N, P).transpose(3, 0, 1, 2, 4),
        "wgu_tail": gu[..., N * P:],
        "wd": np.concatenate([f(L0_ffn_Sd), f(L0_ffn_Wd).reshape(E * FE, H)], axis=0),
        "wproj": np.concatenate([wx[:R].T, np.zeros((H, 1), np.float32), f(L0_ffn_Wr), f(L0_ffn_Wsg), wx[R + N:].T,
                                 wx[R:R + N].T], axis=1).reshape(KC, P, PR).transpose(1, 0, 2),
        "wdt": np.concatenate([f(L0_attn_W_dt).T, f(L0_attn_b_dt)[None]]).reshape(R + 1, KC, P),
        "alog": f(L0_attn_A_log).reshape(KC, P, N).transpose(1, 0, 2).reshape(P, KC * N),
        "dskip": f(L0_attn_D),
        "consts": consts,
        "selectors": selectors,
    }
    arrays = {k: np.ascontiguousarray(v) for k, v in arrays.items()}
    nc = bacc.Bacc("TRN2", target_bir_lowering=False, num_devices=1)
    args = {k: nc.dram_tensor(k, v.shape, mybir.dt.from_np(v.dtype), kind="ExternalInput").ap()
            for k, v in arrays.items()}
    args["out"] = nc.dram_tensor("out", (NB * L, H), F32, kind="ExternalOutput").ap()
    build(nc, **args)
    r = run_bass_kernel_spmd(nc, [arrays], core_ids=[0])
    return r.results[0]["out"].reshape(NB, L, H)
```
